# Optimizing a Trainium2 kernel written in Bass

```python
import numpy as np
import jax
import jax.numpy as jnp

def _softmax(x, axis=-1):
    return jax.nn.softmax(x, axis=axis)

def _gelu(x):
    return jax.nn.gelu(x, approximate=True)

def _silu(x):
    return jax.nn.silu(x)

def _sigmoid(x):
    return jax.nn.sigmoid(x)

def _layernorm(x, axis=-1, eps=1e-05):
    m = jnp.mean(x, axis=axis, keepdims=True)
    v = jnp.var(x, axis=axis, keepdims=True)
    return (x - m) / jnp.sqrt(v + eps)

def _scatter_add(tgt, idx, src, axis=0):
    return tgt.at[idx].add(src)

def _segment_sum(src, seg, n):
    return jax.ops.segment_sum(src, seg, n)
kernel_name = 'mk_gnn_ffn_d1_gnn_r64_161b16'

def setup_inputs(seed: int=0):
    np.random.seed(seed)
    _w = jnp.asarray

    def _rec_inputs():
        import jax
        import jax.numpy as jnp
        _gk = jax.random.key(seed)
        x = -6.415e-05 + 1 * jax.random.normal(jax.random.fold_in(_gk, 1), (10000, 512), jnp.float32)
        src = jax.random.randint(jax.random.fold_in(_gk, 2), (2500,), 0, 10000, jnp.int32)
        dst = jnp.minimum((10000 * jax.random.uniform(jax.random.fold_in(_gk, 3), (2500,)) ** 2.0).astype(jnp.int32), 9999)
        _o = jnp.argsort(dst, stable=True)
        src = src[_o]
        dst = dst[_o]
        return (x, src, dst)
    x, src, dst = _rec_inputs()

    def _L0_gnn_setup():
        import jax, jax.numpy as jnp
        import numpy as np
        N, E, DM, H, DFF = (20000, 10000, 512, 8, 32)
        DK = DM // H

        def _layernorm(x, g, b, eps=1e-05):
            mu = jnp.mean(x, axis=-1, keepdims=True)
            var = jnp.mean(jnp.square(x - mu), axis=-1, keepdims=True)
            return (x - mu) * jax.lax.rsqrt(var + eps) * g + b
        key = jax.random.key(seed)
        ks = jax.random.split(key, 12)
        s = 0.02
        h = jax.random.normal(ks[0], (N, DM), dtype=jnp.float32)
        src = jax.random.randint(ks[1], (E,), 0, N, dtype=jnp.int32)
        dst = jnp.sort(jax.random.randint(ks[2], (E,), 0, N, dtype=jnp.int32))
        return {'h': h, 'src': src, 'dst': dst, 'Wq': jax.random.normal(ks[3], (DM, DM), dtype=jnp.float32) * s, 'Wk': jax.random.normal(ks[4], (DM, DM), dtype=jnp.float32) * s, 'Wv': jax.random.normal(ks[5], (DM, DM), dtype=jnp.float32) * s, 'Wo': jax.random.normal(ks[6], (DM, DM), dtype=jnp.float32) * s, 'ln1_g': jnp.ones((DM,), jnp.float32), 'ln1_b': jnp.zeros((DM,), jnp.float32), 'ln2_g': jnp.ones((DM,), jnp.float32), 'ln2_b': jnp.zeros((DM,), jnp.float32), 'W1': jax.random.normal(ks[7], (DM, DFF), dtype=jnp.float32) * s, 'b1': jnp.zeros((DFF,), jnp.float32), 'W2': jax.random.normal(ks[8], (DFF, DM), dtype=jnp.float32) * s, 'b2': jnp.zeros((DM,), jnp.float32)}
    _L0_gnn_all = _L0_gnn_setup()
    _L0_gnn_in = {k: v for k, v in _L0_gnn_all.items() if k in ('Wq', 'Wk', 'Wv', 'Wo', 'ln1_g', 'ln1_b', 'ln2_g', 'ln2_b', 'W1', 'b1', 'W2', 'b2')}
    del _L0_gnn_all

    def _L0_ffn_setup():
        import jax, jax.numpy as jnp
        import numpy as np
        EPS = 1e-05

        def _bitlinear(x, w):
            w_scale = jnp.clip(jnp.mean(jnp.abs(w)), EPS, None)
            w_q = jnp.clip(jnp.round(w / w_scale), -1.0, 1.0) * w_scale
            w_eff = w + jax.lax.stop_gradient(w_q - w)
            x_scale = 127.0 / jnp.clip(jnp.max(jnp.abs(x), axis=-1, keepdims=True), EPS, None)
            x_q = jnp.clip(jnp.round(x * x_scale), -128.0, 127.0) / x_scale
            x_eff = x + jax.lax.stop_gradient(x_q - x)
            return jnp.einsum('bsi,oi->bso', x_eff, w_eff)

        def _ste_round_clamp_int8(h):
            h_q = jnp.clip(jnp.round(h), -128.0, 127.0)
            return h + jax.lax.stop_gradient(h_q - h)
        key = jax.random.key(seed)
        k1, k2, k3 = jax.random.split(key, 3)
        B, S, D, F = (8, 128, 512, 32)
        x = jax.random.normal(k1, (B, S, D), dtype=jnp.float32)
        w_up = jax.random.normal(k2, (F, D), dtype=jnp.float32) * (1.0 / np.sqrt(D))
        w_down = jax.random.normal(k3, (D, F), dtype=jnp.float32) * (1.0 / np.sqrt(F))
        return {'x': x, 'w_up': w_up, 'w_down': w_down}
    _L0_ffn_all = _L0_ffn_setup()
    _L0_ffn_in = {k: v for k, v in _L0_ffn_all.items() if k in ('w_up', 'w_down')}
    del _L0_ffn_all
    return {'x': x, 'src': src, 'dst': dst, 'L0_gnn_Wq': _L0_gnn_in['Wq'], 'L0_gnn_Wk': _L0_gnn_in['Wk'], 'L0_gnn_Wv': _L0_gnn_in['Wv'], 'L0_gnn_Wo': _L0_gnn_in['Wo'], 'L0_gnn_ln1_g': _L0_gnn_in['ln1_g'], 'L0_gnn_ln1_b': _L0_gnn_in['ln1_b'], 'L0_gnn_ln2_g': _L0_gnn_in['ln2_g'], 'L0_gnn_ln2_b': _L0_gnn_in['ln2_b'], 'L0_gnn_W1': _L0_gnn_in['W1'], 'L0_gnn_b1': _L0_gnn_in['b1'], 'L0_gnn_W2': _L0_gnn_in['W2'], 'L0_gnn_b2': _L0_gnn_in['b2'], 'L0_ffn_w_up': _L0_ffn_in['w_up'], 'L0_ffn_w_down': _L0_ffn_in['w_down']}

def reference(x, src, dst, L0_gnn_Wq, L0_gnn_Wk, L0_gnn_Wv, L0_gnn_Wo, L0_gnn_ln1_g, L0_gnn_ln1_b, L0_gnn_ln2_g, L0_gnn_ln2_b, L0_gnn_W1, L0_gnn_b1, L0_gnn_W2, L0_gnn_b2, L0_ffn_w_up, L0_ffn_w_down):
    import jax
    import jax.numpy as jnp

    def _L0_gnn_ref(h, src, dst, Wq, Wk, Wv, Wo, ln1_g, ln1_b, ln2_g, ln2_b, W1, b1, W2, b2):
        import jax, jax.numpy as jnp
        import numpy as np
        N, E, DM, H, DFF = (20000, 10000, 512, 8, 32)
        DK = DM // H

        def _layernorm(x, g, b, eps=1e-05):
            mu = jnp.mean(x, axis=-1, keepdims=True)
            var = jnp.mean(jnp.square(x - mu), axis=-1, keepdims=True)
            return (x - mu) * jax.lax.rsqrt(var + eps) * g + b
        n = h.shape[0]
        q = (h @ Wq).reshape(n, H, DK)
        k = (h @ Wk).reshape(n, H, DK)
        v = (h @ Wv).reshape(n, H, DK)
        e = jnp.einsum('ehd,ehd->eh', k[src], q[dst]) / np.sqrt(DK).astype(np.float32)
        m = jax.ops.segment_max(e, dst, num_segments=n)
        ex = jnp.exp(e - m[dst])
        z = jax.ops.segment_sum(ex, dst, num_segments=n)
        attn = ex / z[dst]
        a = jax.ops.segment_sum(attn[:, :, None] * v[src], dst, num_segments=n)
        a = a.reshape(n, DM)
        o = a @ Wo
        x = _layernorm(h + o, ln1_g, ln1_b)
        f = jax.nn.relu(x @ W1 + b1) @ W2 + b2
        return _layernorm(x + f, ln2_g, ln2_b)

    def _L0_ffn_ref(x, w_up, w_down):
        import jax, jax.numpy as jnp
        import numpy as np
        EPS = 1e-05

        def _bitlinear(x, w):
            w_scale = jnp.clip(jnp.mean(jnp.abs(w)), EPS, None)
            w_q = jnp.clip(jnp.round(w / w_scale), -1.0, 1.0) * w_scale
            w_eff = w + jax.lax.stop_gradient(w_q - w)
            x_scale = 127.0 / jnp.clip(jnp.max(jnp.abs(x), axis=-1, keepdims=True), EPS, None)
            x_q = jnp.clip(jnp.round(x * x_scale), -128.0, 127.0) / x_scale
            x_eff = x + jax.lax.stop_gradient(x_q - x)
            return jnp.einsum('bsi,oi->bso', x_eff, w_eff)

        def _ste_round_clamp_int8(h):
            h_q = jnp.clip(jnp.round(h), -128.0, 127.0)
            return h + jax.lax.stop_gradient(h_q - h)
        h = _bitlinear(x, w_up)
        h = jax.nn.relu(h)
        h = _ste_round_clamp_int8(h)
        return _bitlinear(h, w_down)
    x = x + _L0_gnn_ref(_layernorm(x, axis=-1), src, dst, L0_gnn_Wq, L0_gnn_Wk, L0_gnn_Wv, L0_gnn_Wo, L0_gnn_ln1_g, L0_gnn_ln1_b, L0_gnn_ln2_g, L0_gnn_ln2_b, L0_gnn_W1, L0_gnn_b1, L0_gnn_W2, L0_gnn_b2)
    x = x + _L0_ffn_ref(_layernorm(x, axis=-1)[None], L0_ffn_w_up, L0_ffn_w_down)[0]
    return x

_drawn_inputs = setup_inputs


def setup_inputs(seed=0):
    import zlib

    import numpy as np

    out = dict(_drawn_inputs(seed))
    spreads = {'L0_gnn_ln1_g': (1.0, 0.2),
     'L0_gnn_ln1_b': (0.0, 0.1),
     'L0_gnn_ln2_g': (1.0, 0.2),
     'L0_gnn_ln2_b': (0.0, 0.1),
     'L0_gnn_b1': (0.0, 1.381),
     'L0_gnn_b2': (0.0, 0.1)}
    factors = {'L0_gnn_Wq': 31.142, 'L0_gnn_Wk': 30.777}
    for name, (base, spread) in spreads.items():
        noise = np.random.default_rng([zlib.crc32(name.encode()), seed]).standard_normal(out[name].shape)
        drawn = base * np.exp(spread * noise) if base else spread * noise
        out[name] = jnp.asarray(drawn.astype(out[name].dtype))
    for name, factor in factors.items():
        out[name] = (out[name] * factor).astype(out[name].dtype)
    return out
```

```python
import concourse.bass as bass
from concourse import mybir
from contextlib import ExitStack



def gnn_ffn_kernel(nc, x, src, dst, Wq, Wk, Wv, Wo, ln1_g, ln1_b, ln2_g, ln2_b, W1, b1, W2, b2, w_up, w_down, out):
    F32, BF16, I32 = mybir.dt.float32, mybir.dt.bfloat16, mybir.dt.int32
    ALU, ACT, AX = mybir.AluOpType, mybir.ActivationFunctionType, mybir.AxisListType
    P = 128
    N, D = x.shape
    E = src.shape[0]
    H, FF = 8, W1.shape[1]
    KC = D // P
    ROWS = 2 * P
    NODE_UNITS = -(-N // ROWS)
    LAST_BASE = N - ROWS
    EDGE_UNITS = -(-E // ROWS)
    ETILES = 2 * EDGE_UNITS
    EPAD = EDGE_UNITS * ROWS
    UNITS = NODE_UNITS + EDGE_UNITS
    EPS = 1e-5
    MAGIC = 1.5 * 2.0 ** 23
    NEG = -3.0e38
    SKIP = 1 << 20
    MSTEP0 = 4
    M_ITERS = EDGE_UNITS
    NSTEP0 = MSTEP0 + 2 * M_ITERS
    N_ITERS = (NODE_UNITS - NSTEP0) // 2
    F_ITERS = (EDGE_UNITS - 2) // 2
    assert NODE_UNITS % 2 == 0 and EDGE_UNITS % 2 == 0 and N_ITERS > 0 and F_ITERS > 0

    es = ExitStack()
    serial = iter(range(1000))
    sb = lambda shape, dt=F32: es.enter_context(nc.sbuf_tensor(f"sb{next(serial)}", shape, dt))
    ps = lambda: es.enter_context(nc.psum_tensor(f"bank{next(serial)}", [P, 512], F32))
    sem = lambda name: es.enter_context(nc.semaphore(name))
    two = lambda shape, dt=F32: [sb(shape, dt), sb(shape, dt)]

    with es:
        ident, ident_bf, ones = sb([P, P]), sb([P, P], BF16), sb([P, P])
        wq_sb, wk_sb, wv_sb = (sb([P, KC, D]) for _ in range(3))
        wo_sb = wk_sb
        w1_sb, w1g, wd_raw = sb([P, KC, FF]), sb([P, KC, FF]), sb([P, KC, FF])
        g1_bc, g2_bc, bln2_bc = sb([P, D]), sb([P, D]), sb([P, D])
        g1_col, bln1_col, b1_col, c1_col = sb([P, KC]), sb([P, KC]), sb([FF, 1]), sb([FF, 1])
        w2e = sb([FF + 1, D])
        wu_q, wd_q = sb([FF, D], BF16), sb([P, KC, 2, FF], BF16)
        wupT, wdT = sb([P, KC, FF], BF16), sb([2 * FF, D], BF16)
        wsum, ws, wsr, wsu127, wsd127 = sb([P, 2]), sb([P, 2]), sb([P, 2]), sb([P, 1]), sb([P, 1])
        neghalf, negmagic, posmagic = sb([P, 4]), sb([P, 1]), sb([P, 1])
        dst_i, nxt_i, src_i, gdst_i, sct_i = (sb([P, ETILES], I32) for _ in range(5))
        notlast = sb([P, ETILES])
        sbias = sb([H, EPAD], BF16)
        headsel, headexp = sb([P, KC, H]), sb([H, KC, P])
        xin, xn, xg1, s, xb, x1 = (two([P, 2, D]) for _ in range(6))
        um = sb([P, 2, D])
        sg = s
        sn, qm, res, junk = sb([P, 2, D]), sb([P, 2, D]), two([P, 2, D]), sb([P, 4, D], BF16)
        brow, wu_raw, wu_t = qm[0:FF + 1, 0, :], qm[0:FF, 1, :], sn[0:FF, 0, :]
        xT, xqT = sb([P, KC, ROWS]), sb([P, KC, ROWS], BF16)
        hTe = two([FF + 1, ROWS])
        q2, q2T = sb([P, 2, FF], BF16), sb([2 * FF, P], BF16)
        st, mv, tR, R = two([P, 2, 6]), two([P, 2, 2]), sb([P, 2]), two([P, 2])
        ssum, mneg, ss2, t2, r2 = two([P, 2]), two([P, 2]), two([P, 2]), sb([P, 2]), two([P, 2])
        xsum, m3neg, ss3, t3, r3 = two([P, 2]), two([P, 2]), two([P, 2]), sb([P, 2]), two([P, 2])
        am, amr, ainv, K, rs1 = sb([P, 2]), sb([P, 2]), sb([P, 2]), two([P, 2]), two([P, 2])
        h1, h2, h3 = (sb([P, 2, FF]) for _ in range(3))
        hmx, hmc, hinv, rs2 = sb([P, 2]), sb([P, 2]), sb([P, 2]), two([P, 2])
        eg = sb([P, 4, D])
        est, emv, etr, er = sb([P, 4, 6]), sb([P, 4, 2]), sb([P, 4]), sb([P, 4])
        hT = sb([P, 2, KC, ROWS])
        kq, prod, vS, wv = two([P, 2, ROWS]), sb([P, KC, ROWS]), sb([P, KC, ROWS]), two([P, ROWS])
        aT = sb([P, KC, EPAD + 1])
        dstrow_i = aT[0:H, 0, :].bitcast(I32)
        mx, zz, dd, wc, rz, bz = (sb([H, ROWS + 1]), sb([H, ROWS + 1]), sb([H, 2, ROWS]), sb([H, 2, ROWS]),
                                  sb([H, ROWS]), sb([H, ROWS]))
        ab = dd
        fst, fmv, ftr, fr = sb([P, 2, 6]), sb([P, 2, 2]), sb([P, 2]), sb([P, 2])
        xg = [eg[:, 0:2, :], eg[:, 2:4, :]]
        y = hT[:, 0].rearrange("p k r -> p (k r)").rearrange("p (j d) -> p j d", j=2)
        aC = hT[:, 1]
        res_e = [t[:].rearrange("p k r -> p (k r)").rearrange("p (j d) -> p j d", j=2) for t in (prod, vS)]
        eidx, gidx, sidx = sb([P, 4], I32), two([P, 2], I32), two([P, 2], I32)
        TP, FB, SMQ, SMZ, EB = [ps(), ps()], [ps(), ps()], ps(), ps(), [ps(), ps()]

        wo_in, w_in, set_v, set_g, set_pe, set_a = (sem(n) for n in ("wo_in", "w_in", "set_v", "set_g", "set_pe", "set_a"))
        xload = [sem("xload0"), sem("xload1")]
        odone = [sem("odone0"), sem("odone1")]
        sdone = [sem("sdone0"), sem("sdone1")]
        A_bn, A_mv, R_t, R_s = sem("A_bn"), sem("A_mv"), sem("R_t"), sem("R_s")
        xn_s, xg1_s, xb_s = sem("xn_s"), sem("xg1_s"), sem("xb_s")
        xt_pe, xT_s, z_s, hT_s, f_s = (sem(n) for n in ("xt_pe", "xT_s", "z_s", "hT_s", "f_s"))
        s_s, mneg_s, sq2_s, t2_s, r2_s, sn_s, sg_s = (sem(n) for n in (
            "s_s", "mneg_s", "sq2_s", "t2_s", "r2_s", "sn_s", "sg_s"))
        x1_s, m3neg_s, um_s, sq3_s, t3_s, r3_s = (sem(n) for n in (
            "x1_s", "m3neg_s", "um_s", "sq3_s", "t3_s", "r3_s"))
        F_c, K_s = sem("F_c"), sem("K_s")
        qm_s, xq_pe, xqT_s, up_s = sem("qm_s"), sem("xq_pe"), sem("xqT_s"), sem("up_s")
        G_c, G_d, q2_s, q2_pe, q2T_s, dn_s, res_s = (sem(n) for n in (
            "G_c", "G_d", "q2_s", "q2_pe", "q2T_s", "dn_s", "res_s"))
        egl, eb_s, emv_s, etr_s, er_s, eh_s = (sem(n) for n in ("egl", "eb_s", "emv_s", "etr_s", "er_s", "eh_s"))
        et_pe, hTe_s, qk_pe, kq_s, prod_s, e_pe = (sem(n) for n in ("et_pe", "eT_s", "qk_pe", "kq_s", "prod_s", "e_pe"))
        sm_c, dd_s, wc_s, ab_s, v_pe, vS_s, bc_pe, wv_s, sc_s = (sem(n) for n in (
            "sm_c", "dd_s", "wc_s", "ab_s", "v_pe", "vS_s", "bc_pe", "wv_s", "sc_s"))
        xgl = [sem("xgl0"), sem("xgl1")]
        fb_s, fmv_s, ftr_s, fr_s, y_s, aC_s, o_pe = (sem(n) for n in (
            "fb_s", "fmv_s", "ftr_s", "fr_s", "y_s", "aC_s", "o_pe"))
        eidx_s, gidx_s, sidx_s = sem("eidx_s"), sem("gidx_s"), sem("sidx_s")
        block = es.enter_context(nc.Block())

        def bc_rows(t, n):
            return t[:].unsqueeze(1).broadcast_to([P, n, D])

        def bc_last(t, n):
            return t[:].unsqueeze(2).broadcast_to([P, 2, n])

        def back(q, par, k):
            n = par - k
            return q + n // 2, n % 2

        def num(q, par):
            return 2 * q + par

        def at_least(eng, sm, value):
            if not (isinstance(value, int) and value <= 0):
                eng.wait_ge(sm, value)

        def live_at(step):
            return lambda k: 0 <= step - k < UNITS

        always = lambda k: True

        @block.sync
        def _(sp):
            col = lambda v: v.rearrange("(k p) -> p k", p=P)
            mat = lambda m: m.rearrange("(k p) f -> p k f", p=P)
            row = lambda v: v.unsqueeze(0)

            def load(q, par, base):
                u = num(q, par)
                at_least(sp, xn_s, 2 * (u - 1))
                at_least(sp, xb_s, u - 1)
                sp.dma_start(xin[par][:], x[base, :].rearrange("(j p) d -> p j d", p=P)).then_inc(xload[par], 16)

            def store(q, par, lo):
                sp.wait_ge(res_s, 2 * num(q, par) + 2)
                for j in range(2):
                    sp.dma_start(out[lo(j), :], res[par][:, j, :]).then_inc(odone[par], 16)

            rows = lambda q, par: bass.ds((2 * q + par) * ROWS, ROWS)
            orow = lambda q, par: (lambda j: bass.ds((2 * q + par) * ROWS + j * P, P))
            load(0, 0, rows(0, 0))
            load(0, 1, rows(0, 1))
            for t, v in ((w1_sb, mat(W1)), (g1_bc, ln1_g.partition_broadcast(P)), (g2_bc, ln2_g.partition_broadcast(P)),
                         (bln2_bc, ln2_b.partition_broadcast(P)), (g1_col, col(ln1_g)), (bln1_col, col(ln1_b)),
                         (b1_col, b1.rearrange("(p k) -> p k", k=1)), (wd_raw, mat(w_down)), (wu_raw, w_up)):
                sp.dma_start(t[:], v, allow_slow_non_contiguous=True).then_inc(w_in, 16)
            sp.dma_start(w2e[0:FF, :], W2[:, :]).then_inc(w_in, 16)
            sp.dma_start(w2e[FF:FF + 1, :], row(b2)).then_inc(w_in, 16)
            sp.dma_start(brow[FF:FF + 1, :], row(ln1_b)).then_inc(w_in, 16)
            sp.wait_ge(set_v, 3)
            full = E // P
            rest = E - full * P
            for t, v in ((dst_i, dst), (src_i, src)):
                sp.dma_start(t[:, 0:full], v[0:full * P].rearrange("(t p) -> p t", p=P),
                             allow_slow_non_contiguous=True).then_inc(w_in, 16)
                sp.dma_start(t[0:rest, full:full + 1], v[full * P:E].rearrange("(p t) -> p t", t=1)).then_inc(w_in, 16)
            sp.dma_start(nxt_i[:, 0:full], dst[1:full * P + 1].rearrange("(t p) -> p t", p=P),
                             allow_slow_non_contiguous=True).then_inc(w_in, 16)
            sp.dma_start(nxt_i[0:rest - 1, full:full + 1],
                         dst[full * P + 1:E].rearrange("(p t) -> p t", t=1)).then_inc(w_in, 16)
            sp.dma_start(dstrow_i[:, 1:E + 1], dst.partition_broadcast(H)).then_inc(w_in, 16)
            for t, v in ((wk_sb, Wk), (wq_sb, Wq), (wv_sb, Wv)):
                sp.dma_start(t[:], mat(v)).then_inc(w_in, 16)

            for step in range(MSTEP0):
                q, par = divmod(step + 2, 2)
                load(q, par, rows(q, par))
                if step >= 3:
                    q, par = divmod(step - 3, 2)
                    store(q, par, orow(q, par))
            with sp.Fori(MSTEP0 // 2, NODE_UNITS // 2 - 2) as i:
                for par in range(2):
                    load(i + 1, par, rows(i + 1, par))
                    qs, ps_ = back(i, par, 3)
                    store(qs, ps_, orow(qs, ps_))
            h = NODE_UNITS // 2 - 2
            load(h + 1, 0, rows(h + 1, 0))
            store(*back(h, 0, 3), orow(*back(h, 0, 3)))
            load(h + 1, 1, bass.ds(LAST_BASE, ROWS))
            sp.wait_ge(qk_pe, 4 * M_ITERS)
            sp.dma_start(wo_sb[:], mat(Wo)).then_inc(wo_in, 16)
            for u in range(NODE_UNITS - 6, NODE_UNITS - 1):
                q, par = divmod(u, 2)
                store(q, par, orow(q, par))
            sp.wait_ge(odone[0], 32 * (NODE_UNITS // 2))
            q, par = divmod(NODE_UNITS - 1, 2)
            store(q, par, lambda j: bass.ds(LAST_BASE + j * P, P))

        @block.vector
        def _(dve):
            V = nc.vector
            V.memset(dst_i[:], -1)
            V.memset(nxt_i[:], -1).then_inc(set_v, 1)
            V.memset(src_i[:], 0).then_inc(set_v, 1)
            V.memset(dstrow_i, -1).then_inc(set_v, 1)
            V.memset(ones[:], 1.0)
            V.memset(neghalf[:], -0.5)
            V.memset(negmagic[:], -MAGIC)
            V.memset(mx[:, 0:1], 0.0)
            V.memset(zz[:, 0:1], 0.0)
            for t in hTe:
                V.memset(t[FF:FF + 1, :], 1.0)
            V.memset(wsum[:], 0.0).then_inc(set_v, 1)
            dve.wait_ge(w_in, 16 * 22)
            dve.wait_ge(set_v, 4)
            V.tensor_reduce(wsum[0:FF, 0:1], wu_raw, AX.X, ALU.add, apply_absolute_value=True)
            V.tensor_reduce(wsum[:, 1:2], wd_raw[:].rearrange("p k f -> p (k f)"), AX.X, ALU.add,
                            apply_absolute_value=True).then_inc(set_v, 1)
            V.tensor_tensor(w2e[FF:FF + 1, :], w2e[FF:FF + 1, :], brow[FF:FF + 1, :], ALU.add)
            for k in range(KC):
                V.tensor_scalar(w1g[:, k, :], w1_sb[:, k, :], g1_col[:, k:k + 1], None, ALU.mult)
            V.tensor_tensor(sbias[:], dstrow_i[:, 1:EPAD + 1], dstrow_i[:, 0:EPAD], ALU.not_equal)
            V.tensor_tensor(notlast[:], nxt_i[:], dst_i[:], ALU.is_equal)
            V.tensor_scalar(gdst_i[:], dst_i[:], 0, None, ALU.max).then_inc(set_v, 1)
            dve.wait_ge(set_v, 6)
            V.memset(sbias[:, 0:1], 1.0)
            V.memset(aT[:, :, 0:1], 0.0)
            V.tensor_scalar(notlast[:], notlast[:], float(SKIP), None, ALU.mult).then_inc(set_v, 1)
            dve.wait_ge(set_v, 7)
            V.tensor_scalar(sbias[:], sbias[:], NEG, None, ALU.mult)
            V.tensor_tensor(sct_i[:], notlast[:], gdst_i[:], ALU.add).then_inc(set_v, 1)
            dve.wait_ge(set_pe, 1)
            V.tensor_scalar(ws[:, 0:1], SMQ[:, 0:1], 1.0 / (FF * D), EPS, ALU.mult, ALU.max)
            V.tensor_scalar(ws[:, 1:2], SMQ[:, 1:2], 1.0 / (FF * D), EPS, ALU.mult, ALU.max)
            V.tensor_tensor(c1_col[:], SMZ[0:FF, 0:1], b1_col[:], ALU.add).then_inc(set_v, 1)
            dve.wait_ge(set_v, 9)
            V.reciprocal(wsr[:], ws[:])
            V.tensor_scalar(wsu127[:], ws[:, 0:1], 1.0 / 127.0, None, ALU.mult)
            V.tensor_scalar(wsd127[:], ws[:, 1:2], 1.0 / 127.0, None, ALU.mult).then_inc(set_v, 1)
            dve.wait_ge(set_v, 10)
            wdf = wd_raw[:].rearrange("p k f -> p (k f)")
            V.tensor_scalar(wu_t, wu_raw, wsr[0:FF, 0:1], MAGIC, ALU.mult, ALU.add)
            V.tensor_scalar(wdf, wdf, wsr[:, 1:2], MAGIC, ALU.mult, ALU.add).then_inc(set_v, 1)
            dve.wait_ge(set_v, 11)
            V.tensor_scalar(wu_t, wu_t, MAGIC, 1.0, ALU.subtract, ALU.min)
            V.tensor_scalar(wdf, wdf, MAGIC, 1.0, ALU.subtract, ALU.min).then_inc(set_v, 1)
            dve.wait_ge(set_v, 12)
            V.tensor_scalar(wu_q[:], wu_t, -1.0, None, ALU.max)
            V.tensor_scalar(wd_q[:, :, 0, :], wd_raw[:], -1.0, None, ALU.max)
            V.tensor_scalar(wd_q[:, :, 1, :], wd_raw[:], -1.0, None, ALU.max).then_inc(set_v, 1)

            def stage_A(q, par):
                u = num(q, par)
                dve.wait_ge(xload[par], 16 * q + 16)
                for j in range(2):
                    V.bn_stats(st[par][:, j, :], xin[par][:, j, :]).then_inc(A_bn, 1)
                for j in range(2):
                    dve.wait_ge(A_bn, 2 * u + 1 + j)
                    dve.nop(nofuse=True)
                    V.bn_aggr(mv[par][:, j, :], st[par][:, j, :]).then_inc(A_mv, 1)

            def stage_A0(q, par, k):
                dve.wait_ge(xgl[par], 32 * (q - NODE_UNITS // 2) + 32)
                for j in range(2):
                    V.bn_stats(fst[:, j, :], xg[par][:, j, :]).then_inc(fb_s, 1)
                for j in range(2):
                    dve.wait_ge(fb_s, 2 * k + 1 + j)
                    dve.nop(nofuse=True)
                    V.bn_aggr(fmv[:, j, :], fst[:, j, :]).then_inc(fmv_s, 1)

            def stage_A_edge(q, par, k):
                u = num(q, par)
                dve.wait_ge(fr_s, k + 1)
                dve.wait_ge(o_pe, k + 1)
                for j in range(2):
                    V.scalar_tensor_tensor(y[:, j, :], xg[par][:, j, :], fr[:, j:j + 1], EB[j][:], ALU.mult,
                                           ALU.add).then_inc(y_s, 1)
                for j in range(2):
                    dve.wait_ge(y_s, 2 * k + 1 + j)
                    V.bn_stats(st[par][:, j, :], y[:, j, :]).then_inc(A_bn, 1)
                for j in range(2):
                    dve.wait_ge(A_bn, 2 * u + 1 + j)
                    dve.nop(nofuse=True)
                    V.bn_aggr(mv[par][:, j, :], st[par][:, j, :]).then_inc(A_mv, 1)

            def stage_B(q, par, rows):
                u = num(q, par)
                dve.wait_ge(R_s, u + 1)
                at_least(dve, xg1_s, u - 1)
                at_least(dve, xt_pe, 2 * (u - 1))
                for j in range(2):
                    V.tensor_scalar(xn[par][:, j, :], rows[:, j, :], mv[par][:, j, 0:1], R[par][:, j:j + 1],
                                    ALU.subtract, ALU.mult).then_inc(xn_s, 1)

            def stage_C(q, par):
                u = num(q, par)
                dve.wait_ge(xg1_s, u + 1)
                at_least(dve, sq2_s, 2 * (u - 1))
                for j in range(2):
                    dve.wait_ge(f_s, 2 * u + 1 + j)
                    V.scalar_tensor_tensor(s[par][:, j, :], FB[j][:], 1.0, xg1[par][:, j, :], ALU.mult, ALU.add,
                                           accum_out=ssum[par][:, j:j + 1]).then_inc(s_s, 1)
                dve.wait_ge(s_s, 2 * u + 2)
                V.tensor_scalar(mneg[par][:], ssum[par][:], -1.0 / D, None, ALU.mult).then_inc(mneg_s, 1)

            def stage_D(q, par):
                u = num(q, par)
                dve.wait_ge(r2_s, u + 1)
                at_least(dve, sg_s, u)
                for j in range(2):
                    V.tensor_scalar(sn[:, j, :], s[par][:, j, :], mneg[par][:, j:j + 1], r2[par][:, j:j + 1],
                                    ALU.add, ALU.mult).then_inc(sn_s, 1)

            def stage_E(q, par):
                u = num(q, par)
                dve.wait_ge(sg_s, u + 1)
                dve.wait_ge(xb_s, u + 1)
                at_least(dve, res_s, 2 * (u - 1))
                for j in range(2):
                    V.scalar_tensor_tensor(x1[par][:, j, :], sg[par][:, j, :], 1.0, xb[par][:, j, :], ALU.mult,
                                           ALU.add, accum_out=xsum[par][:, j:j + 1]).then_inc(x1_s, 1)
                dve.wait_ge(x1_s, 2 * u + 2)
                V.tensor_scalar(m3neg[par][:], xsum[par][:], -1.0 / D, None, ALU.mult).then_inc(m3neg_s, 1)

            def stage_F(q, par):
                u = num(q, par)
                dve.wait_ge(um_s, 2 * u + 2)
                V.tensor_reduce(am[:], um[:], AX.X, ALU.max, apply_absolute_value=True).then_inc(F_c, 1)
                dve.wait_ge(F_c, 4 * u + 1)
                dve.wait_ge(r3_s, u + 1)
                V.tensor_tensor(amr[:], am[:], r3[par][:], ALU.mult).then_inc(F_c, 1)
                dve.wait_ge(F_c, 4 * u + 2)
                V.tensor_scalar(amr[:], amr[:], EPS, None, ALU.max).then_inc(F_c, 1)
                dve.wait_ge(F_c, 4 * u + 3)
                V.reciprocal(ainv[:], amr[:])
                V.tensor_scalar(rs1[par][:], amr[:], wsu127[:], None, ALU.mult).then_inc(F_c, 1)
                dve.wait_ge(F_c, 4 * u + 4)
                V.scalar_tensor_tensor(K[par][:], ainv[:], 127.0, r3[par][:], ALU.mult, ALU.mult).then_inc(K_s, 1)

            def stage_G(q, par):
                u = num(q, par)
                g = 6 * u
                dve.wait_ge(up_s, u + 1)
                V.scalar_tensor_tensor(h1[:], SMQ[:, 0:2 * FF].rearrange("p (j f) -> p j f", j=2), 0.0,
                                       bc_last(rs1[par], FF), ALU.max, ALU.mult).then_inc(G_c, 1)
                dve.wait_ge(G_c, g + 1)
                V.tensor_scalar(h2[:], h1[:], 127.0, MAGIC, ALU.min, ALU.add).then_inc(G_c, 1)
                dve.wait_ge(G_c, g + 2)
                V.tensor_scalar(h3[:], h2[:], MAGIC, None, ALU.subtract).then_inc(G_c, 1)
                dve.wait_ge(G_c, g + 3)
                V.tensor_reduce(hmx[:], h3[:], AX.X, ALU.max).then_inc(G_c, 1)
                dve.wait_ge(G_c, g + 4)
                V.tensor_scalar(hmc[:], hmx[:], EPS, None, ALU.max).then_inc(G_c, 1)
                dve.wait_ge(G_c, g + 5)
                V.tensor_scalar(rs2[par][:], hmc[:], wsd127[:], None, ALU.mult)
                V.reciprocal(hinv[:], hmc[:]).then_inc(G_c, 1)
                dve.wait_ge(G_c, g + 6)
                V.scalar_tensor_tensor(h1[:], bc_last(hinv, FF), 127.0, h3[:], ALU.mult, ALU.mult).then_inc(G_d, 1)
                dve.wait_ge(G_d, u + 1)
                at_least(dve, q2_pe, u)
                V.tensor_scalar(q2[:], h1[:], MAGIC, MAGIC, ALU.add, ALU.subtract).then_inc(q2_s, 1)

            def stage_H(q, par, edge):
                u = num(q, par)
                if edge:
                    at_least(dve, sidx_s, u - NODE_UNITS)
                else:
                    at_least(dve, odone[par], 32 * q)
                dest = (res_e if edge else res)[par]
                for j in range(2):
                    dve.wait_ge(dn_s, 2 * u + 1 + j)
                    V.scalar_tensor_tensor(dest[:, j, :], FB[j][:], rs2[par][:, j:j + 1], x1[par][:, j, :],
                                           ALU.mult, ALU.add).then_inc(res_s, 1)

            def step(q, par, live=always, k=None, edge_result=False, gaps={}):
                gap = lambda name: gaps.get(name, lambda: None)()
                if live(0):
                    stage_A(q, par) if k is None else stage_A0(q, par, k)
                gap("A")
                if live(1):
                    stage_C(*back(q, par, 1))
                if live(2):
                    stage_E(*back(q, par, 2))
                if live(0):
                    if k is not None:
                        stage_A_edge(q, par, k)
                    stage_B(q, par, xin[par] if k is None else y)
                gap("B")
                if live(3):
                    stage_G(*back(q, par, 3))
                if live(1):
                    stage_D(*back(q, par, 1))
                if live(2):
                    stage_F(*back(q, par, 2))
                if live(3):
                    stage_H(*back(q, par, 3), edge_result)
                gap("H")

            def edge_stats(i):
                dve.wait_ge(egl, 64 * i + 64)
                for j in range(4):
                    V.bn_stats(est[:, j, :], eg[:, j, :]).then_inc(eb_s, 1)
                for j in range(4):
                    dve.wait_ge(eb_s, 4 * i + 1 + j)
                    dve.nop(nofuse=True)
                    V.bn_aggr(emv[:, j, :], est[:, j, :]).then_inc(emv_s, 1)

            def edge_norm(i):
                dve.wait_ge(er_s, i + 1)
                for j in range(4):
                    V.tensor_scalar(eg[:, j, :], eg[:, j, :], emv[:, j, 0:1], er[:, j:j + 1], ALU.subtract,
                                    ALU.mult).then_inc(eh_s, 1)

            def edge_softmax(i):
                c = 5 * i
                sbw = sbias[:, bass.ds(i * ROWS, ROWS)]
                e = SMZ[0:H, 0:ROWS]
                dve.wait_ge(e_pe, i + 1)
                V.tensor_tensor_scan(mx[:, 1:], sbw, e, mx[:, 0:1], ALU.add, ALU.max).then_inc(sm_c, 1)
                dve.wait_ge(sm_c, c + 1)
                V.tensor_tensor(dd[:, 0, :], e, mx[:, 1:], ALU.subtract).then_inc(dd_s, 1)
                V.tensor_tensor(dd[:, 1, :], mx[:, 0:ROWS], mx[:, 1:], ALU.subtract).then_inc(sm_c, 1)
                dve.wait_ge(sm_c, c + 2)
                V.tensor_tensor(dd[:, 1, :], dd[:, 1, :], sbw, ALU.min).then_inc(dd_s, 1)
                V.tensor_copy(mx[:, 0:1], mx[:, ROWS:ROWS + 1])
                dve.wait_ge(wc_s, i + 1)
                V.tensor_tensor_scan(zz[:, 1:], wc[:, 1, :], wc[:, 0, :], zz[:, 0:1], ALU.mult,
                                     ALU.add).then_inc(sm_c, 1)
                dve.wait_ge(sm_c, c + 3)
                V.reciprocal(rz[:], zz[:, 1:])
                V.tensor_tensor(bz[:], wc[:, 1, :], zz[:, 0:ROWS], ALU.mult).then_inc(sm_c, 1)
                dve.wait_ge(sm_c, c + 4)
                V.tensor_copy(zz[:, 0:1], zz[:, ROWS:ROWS + 1])
                at_least(dve, bc_pe, 4 * i)
                V.tensor_tensor(ab[:, 0, :], wc[:, 0, :], rz[:], ALU.mult)
                V.tensor_tensor(ab[:, 1, :], bz[:], rz[:], ALU.mult).then_inc(sm_c, 1)

            def edge_scan(i, m):
                dve.wait_ge(vS_s, 2 * i + 1 + m // 2)
                dve.wait_ge(bc_pe, 4 * i + 1 + m)
                V.tensor_tensor(wv[m % 2][:], EB[m % 2][:, 0:ROWS], vS[:, m, :], ALU.mult).then_inc(wv_s, 1)
                dve.wait_ge(wv_s, 4 * i + 1 + m)
                V.tensor_tensor_scan(aT[:, m, bass.ds(i * ROWS + 1, ROWS)], EB[m % 2][:, ROWS:2 * ROWS], wv[m % 2][:],
                                     aT[:, m, bass.ds(i * ROWS, 1)], ALU.mult, ALU.add).then_inc(sc_s, 1)

            for t in range(MSTEP0):
                step(*divmod(t, 2), live_at(t))

            def m_body(i):
                edge_stats(i)
                step(MSTEP0 // 2 + i, 0, gaps={"A": lambda: edge_norm(i)})
                step(MSTEP0 // 2 + i, 1, gaps={"B": lambda: edge_softmax(i),
                                               "H": lambda: [edge_scan(i, m) for m in range(KC)]})

            m_body(0)
            with dve.Fori(1, M_ITERS) as i:
                m_body(i)
            with dve.Fori(NSTEP0 // 2, NODE_UNITS // 2) as i:
                for par in range(2):
                    step(i, par)
            for t in range(NODE_UNITS, NODE_UNITS + 4):
                step(*divmod(t, 2), k=t - NODE_UNITS, edge_result=t >= NODE_UNITS + 3)
            with dve.Fori(2, F_ITERS) as i:
                for par in range(2):
                    step(NODE_UNITS // 2 + i, par, k=2 * i + par, edge_result=True)
            for t in range(UNITS - 2, UNITS + 3):
                step(*divmod(t, 2), live_at(t), k=t - NODE_UNITS, edge_result=True)

        @block.scalar
        def _(act):
            A = nc.scalar
            act.wait_ge(set_pe, 2)
            A.activation(wupT[:].rearrange("p k f -> p (k f)"), TP[0][:, 0:KC * FF // 2].bitcast(BF16), ACT.Copy)
            A.activation(wdT[:], TP[1][0:2 * FF, 0:D // 2].bitcast(BF16), ACT.Copy).then_inc(set_a, 1)

            def quantise(q, par):
                u = num(q, par)
                act.wait_ge(K_s, u + 1)
                at_least(act, xq_pe, 2 * u)
                for j in range(2):
                    A.activation(qm[:, j, :], um[:, j, :], ACT.Identity, bias=posmagic[:],
                                 scale=K[par][:, j:j + 1]).then_inc(qm_s, 1)
                at_least(act, up_s, u)
                for b in range(2):
                    act.wait_ge(xq_pe, 2 * u + 1 + b)
                    A.activation(xqT[:, 2 * b:2 * b + 2, :].rearrange("p k r -> p (k r)"), TP[b][:], ACT.Identity,
                                 bias=negmagic[:]).then_inc(xqT_s, 1)

            def square_s(q, par):
                u = num(q, par)
                act.wait_ge(mneg_s, u + 1)
                for j in range(2):
                    A.activation(junk[:, j, :], s[par][:, j, :], ACT.Square, bias=mneg[par][:, j:j + 1],
                                 accum_out=ss2[par][:, j:j + 1]).then_inc(sq2_s, 1)

            def centre_x1(q, par):
                u = num(q, par)
                act.wait_ge(m3neg_s, u + 1)
                for j in range(2):
                    A.activation(um[:, j, :], x1[par][:, j, :], ACT.Identity,
                                 bias=m3neg[par][:, j:j + 1]).then_inc(um_s, 1)
                for j in range(2):
                    A.activation(junk[:, 2 + j, :], x1[par][:, j, :], ACT.Square, bias=m3neg[par][:, j:j + 1],
                                 accum_out=ss3[par][:, j:j + 1]).then_inc(sq3_s, 1)

            def evict_xT(q, par):
                u = num(q, par)
                at_least(act, z_s, u)
                for b in range(2):
                    act.wait_ge(xt_pe, 2 * u + 1 + b)
                    A.activation(xT[:, 2 * b:2 * b + 2, :].rearrange("p k r -> p (k r)"), TP[b][:],
                                 ACT.Copy).then_inc(xT_s, 1)

            def evict_q2T(q, par):
                act.wait_ge(q2_pe, num(q, par) + 1)
                at_least(act, dn_s, 2 * num(q, par))
                A.activation(q2T[:], SMQ[0:2 * FF, 64:64 + P // 2].bitcast(BF16), ACT.Copy).then_inc(q2T_s, 1)

            def relu(q, par):
                u = num(q, par)
                act.wait_ge(z_s, u + 1)
                at_least(act, f_s, 2 * (u - 1))
                A.activation(hTe[par][0:FF, :], SMZ[0:FF, 0:ROWS], ACT.Relu, bias=c1_col[:]).then_inc(hT_s, 1)

            def step(q, par, live=always, gaps={}):
                gap = lambda name: gaps.get(name, lambda: None)()
                if live(3):
                    quantise(*back(q, par, 3))
                gap("up")
                if live(1):
                    square_s(*back(q, par, 1))
                if live(2):
                    centre_x1(*back(q, par, 2))
                if live(0):
                    evict_xT(q, par)
                gap("xT")
                if live(3):
                    evict_q2T(*back(q, par, 3))
                gap("q2T")
                if live(0):
                    relu(q, par)
                gap("relu")

            def edge_hT(i):
                for r in range(4):
                    act.wait_ge(et_pe, 4 * i + 1 + r)
                    A.activation(hT[:, r // 2, 2 * (r % 2):2 * (r % 2) + 2, :].rearrange("p k r -> p (k r)"),
                                 EB[r % 2][:], ACT.Copy).then_inc(hTe_s, 1)

            def edge_kq(i, m):
                act.wait_ge(qk_pe, 4 * i + 1 + m)
                at_least(act, prod_s, 4 * i + max(m - 1, 0))
                A.activation(kq[m % 2][:].rearrange("p s r -> p (s r)"), EB[m % 2][:], ACT.Copy).then_inc(kq_s, 1)

            def edge_v(i, r):
                act.wait_ge(v_pe, 2 * i + 1 + r)
                at_least(act, wv_s, 4 * i)
                A.activation(vS[:, 2 * r:2 * r + 2, :].rearrange("p k r -> p (k r)"), EB[r][:],
                             ACT.Copy).then_inc(vS_s, 1)

            def edge_exp(i):
                act.wait_ge(dd_s, 2 * i + 2)
                A.activation(wc[:].rearrange("p s r -> p (s r)"), dd[:].rearrange("p s r -> p (s r)"), ACT.Exp,
                             scale=float(D // H) ** -0.5).then_inc(wc_s, 1)

            act.wait_ge(set_v, 13)
            for t in range(MSTEP0):
                step(*divmod(t, 2), live_at(t))

            def m_body(i):
                step(MSTEP0 // 2 + i, 0, gaps={"up": lambda: edge_hT(i), "xT": lambda: edge_kq(i, 0),
                                               "q2T": lambda: edge_kq(i, 1),
                                               "relu": lambda: (edge_kq(i, 2), edge_kq(i, 3))})
                step(MSTEP0 // 2 + i, 1, gaps={"up": lambda: edge_v(i, 0), "xT": lambda: (edge_v(i, 1), edge_exp(i))})

            m_body(0)
            with act.Fori(1, M_ITERS) as i:
                m_body(i)
            with act.Fori(NSTEP0 // 2, UNITS // 2) as i:
                for par in range(2):
                    step(i, par)
            for t in range(UNITS, UNITS + 3):
                step(*divmod(t, 2), live_at(t))

        @block.gpsimd
        def _(pool):
            G = nc.gpsimd
            G.memset(posmagic[:], MAGIC)
            G.memset(ident[:], 0.0)
            G.memset(headsel[:], 0.0)
            G.memset(headexp[:], 1.0).then_inc(set_g, 1)
            pool.wait_ge(set_g, 1)
            G.affine_select(out=ident[:], in_=ident[:], compare_op=ALU.not_equal, fill=1.0, base=0,
                            pattern=[[-1, P]], channel_multiplier=1).then_inc(set_g, 1)
            pool.wait_ge(set_g, 2)
            half = P // 2
            for r in range(2):
                G.affine_select(out=headsel[r * half:(r + 1) * half], in_=headsel[r * half:(r + 1) * half],
                                compare_op=ALU.not_equal, fill=1.0, base=-r, pattern=[[-2, KC], [1, H]],
                                channel_multiplier=0).then_inc(set_g, 1)
                pool.wait_ge(set_g, 3 + r)
            G.affine_select(out=headexp[:], in_=headexp[:], compare_op=ALU.is_ge, fill=0.0, base=0,
                            pattern=[[P, KC], [1, P]], channel_multiplier=-half).then_inc(set_g, 1)
            pool.wait_ge(set_g, 5)
            G.affine_select(out=headexp[:], in_=headexp[:], compare_op=ALU.is_ge, fill=0.0, base=half - 1,
                            pattern=[[-P, KC], [-1, P]], channel_multiplier=half)
            G.tensor_copy(ident_bf[:], ident[:]).then_inc(set_g, 1)
            pool.wait_ge(set_v, 13)

            def rows_scale(q, par, node):
                u = num(q, par)
                pool.wait_ge(A_mv, 2 * u + 2)
                pool.nop(nofuse=True)
                if node:
                    G.tensor_scalar(tR[:], mv[par][:, :, 1], 1.0 + EPS, EPS * EPS, ALU.mult, ALU.add).then_inc(R_t, 1)
                else:
                    G.tensor_scalar(tR[:], mv[par][:, :, 1], 1.0, EPS, ALU.mult, ALU.add).then_inc(R_t, 1)
                pool.wait_ge(R_t, u + 1)
                G.tensor_tensor(R[par][:], tR[:], neghalf[:, 0:2], ALU.pow).then_inc(R_s, 1)

            def add_b(q, par, rows):
                u = num(q, par)
                at_least(pool, x1_s, 2 * (u - 1))
                G.tensor_tensor(xb[par][:], rows[:], bc_rows(bln2_bc, 2), ALU.add).then_inc(xb_s, 1)

            def s_scale(q, par):
                u = num(q, par)
                pool.wait_ge(sq2_s, 2 * u + 2)
                pool.nop(nofuse=True)
                G.tensor_scalar(t2[:], ss2[par][:], 1.0 / D, EPS, ALU.mult, ALU.add).then_inc(t2_s, 1)
                pool.wait_ge(t2_s, u + 1)
                G.tensor_tensor(r2[par][:], t2[:], neghalf[:, 0:2], ALU.pow).then_inc(r2_s, 1)

            def gain1(q, par):
                u = num(q, par)
                pool.wait_ge(xn_s, 2 * u + 2)
                at_least(pool, s_s, 2 * (u - 1))
                G.tensor_tensor(xg1[par][:], xn[par][:], bc_rows(g1_bc, 2), ALU.mult).then_inc(xg1_s, 1)

            def x1_scale(q, par):
                u = num(q, par)
                pool.wait_ge(sq3_s, 2 * u + 2)
                pool.nop(nofuse=True)
                G.tensor_scalar(t3[:], ss3[par][:], 1.0 / D, EPS, ALU.mult, ALU.add).then_inc(t3_s, 1)
                pool.wait_ge(t3_s, u + 1)
                G.tensor_tensor(r3[par][:], t3[:], neghalf[:, 0:2], ALU.pow).then_inc(r3_s, 1)

            def gain2(q, par):
                u = num(q, par)
                pool.wait_ge(sn_s, 2 * u + 2)
                at_least(pool, x1_s, 2 * (u - 1))
                G.tensor_tensor(sg[par][:], sn[:], bc_rows(g2_bc, 2), ALU.mult).then_inc(sg_s, 1)

            def step(q, par, live=always, k=None, gaps={}):
                gap = lambda name: gaps.get(name, lambda: None)()
                if live(0):
                    if k is None:
                        rows_scale(q, par, True)
                        add_b(q, par, xin[par])
                    else:
                        edge_row_scale(k)
                        add_b(q, par, xg[par])
                        rows_scale(q, par, False)
                gap("R")
                if live(1):
                    s_scale(*back(q, par, 1))
                gap("r2")
                if live(0):
                    gain1(q, par)
                gap("g1")
                if live(2):
                    x1_scale(*back(q, par, 2))
                gap("r3")
                if live(1):
                    gain2(*back(q, par, 1))
                gap("g2")

            def gather_edges(i):
                at_least(pool, et_pe, 4 * i)
                G.tensor_copy(eidx[:, 0:2], src_i[:, bass.ds(2 * i, 2)])
                G.tensor_copy(eidx[:, 2:4], gdst_i[:, bass.ds(2 * i, 2)]).then_inc(eidx_s, 1)
                pool.wait_ge(eidx_s, i + 1)
                pool.nop(nofuse=True)
                for t in range(4):
                    G.indirect_dma_start(eg[:, t, :], None, x[:, :],
                                         bass.IndirectOffsetOnAxis(ap=eidx[:, t:t + 1], axis=0)).then_inc(egl, 16)

            def edge_scale(i):
                pool.wait_ge(emv_s, 4 * i + 4)
                pool.nop(nofuse=True)
                G.tensor_scalar(etr[:], emv[:, :, 1], 1.0, EPS, ALU.mult, ALU.add).then_inc(etr_s, 1)
                pool.wait_ge(etr_s, i + 1)
                G.tensor_tensor(er[:], etr[:], neghalf[:], ALU.pow).then_inc(er_s, 1)

            def edge_prod(i, m):
                pool.wait_ge(kq_s, 4 * i + 1 + m)
                at_least(pool, e_pe, i)
                G.tensor_tensor(prod[:, m, :], kq[m % 2][:, 0, :], kq[m % 2][:, 1, :], ALU.mult).then_inc(prod_s, 1)

            def gather_dst(par, k):
                G.tensor_copy(gidx[par][:], gdst_i[:, bass.ds(2 * k, 2)]).then_inc(gidx_s, 1)
                pool.wait_ge(gidx_s, k + 1)
                pool.nop(nofuse=True)
                for j in range(2):
                    G.indirect_dma_start(xg[par][:, j, :], None, x[:, :],
                                         bass.IndirectOffsetOnAxis(ap=gidx[par][:, j:j + 1], axis=0)
                                         ).then_inc(xgl[par], 16)

            def edge_row_scale(k):
                pool.wait_ge(fmv_s, 2 * k + 2)
                pool.nop(nofuse=True)
                G.tensor_scalar(ftr[:], fmv[:, :, 1], 1.0, EPS, ALU.mult, ALU.add).then_inc(ftr_s, 1)
                pool.wait_ge(ftr_s, k + 1)
                G.tensor_tensor(fr[:], ftr[:], neghalf[:, 0:2], ALU.pow).then_inc(fr_s, 1)

            def copy_aT(k):
                at_least(pool, o_pe, k)
                G.tensor_copy(aC[:], aT[:, :, bass.ds(k * ROWS + 1, ROWS)]).then_inc(aC_s, 1)

            def scatter(h, par):
                k = 2 * h + par
                pool.wait_ge(res_s, 2 * (NODE_UNITS + k) + 2)
                at_least(pool, sdone[1 - par], 32 * (h + par))
                G.tensor_copy(sidx[par][:], sct_i[:, bass.ds(2 * k, 2)]).then_inc(sidx_s, 1)
                pool.wait_ge(sidx_s, k + 1)
                pool.nop(nofuse=True)
                for j in range(2):
                    G.indirect_dma_start(out[:, :], bass.IndirectOffsetOnAxis(ap=sidx[par][:, j:j + 1], axis=0),
                                         res_e[par][:, j, :], None, bounds_check=N - 1,
                                         oob_is_err=False).then_inc(sdone[par], 16)

            gather_edges(0)
            for t in range(MSTEP0):
                step(*divmod(t, 2), live_at(t))

            def m_body(i, more):
                edge_scale(i)
                step(MSTEP0 // 2 + i, 0, gaps={"g1": lambda: edge_prod(i, 0), "r3": lambda: edge_prod(i, 1),
                                               "g2": lambda: (edge_prod(i, 2), edge_prod(i, 3))})
                if more:
                    gather_edges(i + 1)
                step(MSTEP0 // 2 + i, 1)

            m_body(0, True)
            with pool.Fori(1, M_ITERS - 1) as i:
                m_body(i, True)
            m_body(M_ITERS - 1, False)
            with pool.Fori(NSTEP0 // 2, NODE_UNITS // 2) as i:
                for par in range(2):
                    step(i, par)
            NH = NODE_UNITS // 2
            pool.wait_ge(sc_s, 4 * M_ITERS)
            copy_aT(0)
            gather_dst(0, 0)
            gather_dst(1, 1)

            def f_step(h, par, has_next, has_gather):
                k = 2 * h + par
                def next_inputs():
                    if has_next:
                        copy_aT(k + 1)
                def next_rows():
                    if has_gather:
                        gather_dst(par, k + 2)
                step(NH + h, par, k=k, gaps={"R": next_inputs, "g1": next_rows})

            for k in range(4):
                f_step(*divmod(k, 2), True, True)
            pool.wait_ge(odone[0], 32 * (NODE_UNITS // 2))
            pool.wait_ge(odone[1], 32 * (NODE_UNITS // 2))
            for par in range(2):
                scatter(0, par)
                f_step(2, par, True, True)
            for i in range(3, F_ITERS):
                for par in range(2):
                    scatter(i - 2, par)
                    f_step(i, par, True, True)
            for k in range(2 * F_ITERS, EDGE_UNITS + 3):
                h, par = divmod(k, 2)
                if k - 4 < EDGE_UNITS:
                    scatter(h - 2, par)
                if k < EDGE_UNITS:
                    f_step(h, par, k + 1 < EDGE_UNITS, k + 2 < EDGE_UNITS)
                else:
                    step(NH + h, par, live_at(NODE_UNITS + k))
            scatter(EDGE_UNITS // 2 - 1, 1)
            for par in range(2):
                pool.wait_ge(sdone[par], 32 * (EDGE_UNITS // 2))

        @block.tensor
        def _(pe):
            T = nc.tensor
            pe.wait_ge(set_g, 6)
            pe.wait_ge(set_v, 6)
            T.matmul(SMQ[:, 0:2], ones[:], wsum[:], start=True, stop=True)
            for k in range(KC):
                last = T.matmul(SMZ[0:FF, 0:1], w1_sb[:, k, :], bln1_col[:, k:k + 1], start=(k == 0), stop=(k == KC - 1))
            last.then_inc(set_pe, 1)
            pe.wait_ge(set_v, 13)
            for k in range(KC):
                T.transpose(TP[0][:, k * FF // 2:(k + 1) * FF // 2].bitcast(BF16), wu_q[:, k * P:(k + 1) * P],
                            ident_bf[0:FF, 0:FF])
            for k in range(KC):
                last = T.transpose(TP[1][0:2 * FF, k * P // 2:(k + 1) * P // 2].bitcast(BF16),
                                   wd_q[:, k, :, :].rearrange("p a f -> p (a f)"), ident_bf[:])
            last.then_inc(set_pe, 1)
            pe.wait_ge(set_a, 1)

            def transpose_xq(q, par):
                u = num(q, par)
                pe.wait_ge(qm_s, 2 * u + 2)
                for b in range(2):
                    pe.wait_ge(xT_s, 2 * (u + 2) + 1 + b) if not isinstance(u, int) or u + 2 < UNITS else pe.wait_ge(
                        xT_s, 2 * UNITS)
                    for kk in range(2):
                        k = 2 * b + kk
                        for j in range(2):
                            last = T.transpose(TP[b][:, kk * ROWS + j * P:kk * ROWS + (j + 1) * P],
                                               qm[:, j, k * P:(k + 1) * P], ident[:])
                    last.then_inc(xq_pe, 1)

            def up(q, par):
                u = num(q, par)
                pe.wait_ge(xqT_s, 2 * u + 2)
                at_least(pe, q2T_s, u)
                for j in range(2):
                    for k in range(KC):
                        last = T.matmul(SMQ[:, j * FF:(j + 1) * FF], xqT[:, k, j * P:(j + 1) * P], wupT[:, k, :],
                                        start=(k == 0), stop=(k == KC - 1))
                last.then_inc(up_s, 1)

            def transpose_x(q, par, quant):
                u = num(q, par)
                pe.wait_ge(xn_s, 2 * u + 2)
                for b in range(2):
                    if quant:
                        pe.wait_ge(xqT_s, 2 * (u - 3) + 1 + b)
                    else:
                        at_least(pe, xT_s, 2 * (u - 1) + 1 + b)
                    for kk in range(2):
                        k = 2 * b + kk
                        for j in range(2):
                            last = T.transpose(TP[b][:, kk * ROWS + j * P:kk * ROWS + (j + 1) * P],
                                               xn[par][:, j, k * P:(k + 1) * P], ident[:])
                    last.then_inc(xt_pe, 1)

            def transpose_q2(q, par):
                u = num(q, par)
                pe.wait_ge(q2_s, u + 1)
                pe.nop(nofuse=True)
                T.transpose(SMQ[0:2 * FF, 64:64 + P // 2].bitcast(BF16), q2[:].rearrange("p j f -> p (j f)"),
                            ident_bf[:]).then_inc(q2_pe, 1)

            def hidden(q, par, e_done):
                u = num(q, par)
                pe.wait_ge(xT_s, 2 * u + 2)
                at_least(pe, hT_s, u)
                at_least(pe, sm_c, e_done)
                for k in range(KC):
                    last = T.matmul(SMZ[0:FF, 0:ROWS], w1g[:, k, :], xT[:, k, :], start=(k == 0), stop=(k == KC - 1))
                last.then_inc(z_s, 1)

            def down(q, par):
                u = num(q, par)
                pe.wait_ge(q2T_s, u + 1)
                at_least(pe, s_s, 2 * (u + 2) + 2) if not isinstance(u, int) or u + 2 < UNITS else pe.wait_ge(
                    s_s, 2 * UNITS)
                for j in range(2):
                    T.matmul(FB[j][:], q2T[j * FF:(j + 1) * FF, :], wdT[j * FF:(j + 1) * FF, :], start=True,
                             stop=True).then_inc(dn_s, 1)

            def ffn(q, par, after_down):
                u = num(q, par)
                pe.wait_ge(hT_s, u + 1)
                for j in range(2):
                    if after_down:
                        pe.wait_ge(res_s, 2 * (u - 3) + 1 + j)
                    else:
                        at_least(pe, s_s, 2 * (u - 1) + 1 + j)
                    T.matmul(FB[j][:], hTe[par][:, j * P:(j + 1) * P], w2e[:], start=True, stop=True).then_inc(f_s, 1)

            def step(q, par, live=always, e_done=0, gaps={}):
                gap = lambda name: gaps.get(name, lambda: None)()
                if live(3):
                    transpose_xq(*back(q, par, 3))
                    up(*back(q, par, 3))
                gap("up")
                if live(0):
                    transpose_x(q, par, live(3))
                gap("xT")
                if live(3):
                    transpose_q2(*back(q, par, 3))
                gap("q2T")
                if live(0):
                    hidden(q, par, e_done)
                gap("z")
                if live(3):
                    down(*back(q, par, 3))
                gap("down")
                if live(0):
                    ffn(q, par, live(3))
                gap("f")

            def edge_transpose(i):
                pe.wait_ge(eh_s, 4 * i + 4)
                for r in range(4):
                    side, b = divmod(r, 2)
                    if r < 2:
                        at_least(pe, sc_s, 4 * i)
                    else:
                        pe.wait_ge(hTe_s, 4 * i - 1 + r)
                    for kk in range(2):
                        k = 2 * b + kk
                        for j in range(2):
                            last = T.transpose(EB[r % 2][:, kk * ROWS + j * P:kk * ROWS + (j + 1) * P],
                                               eg[:, 2 * side + j, k * P:(k + 1) * P], ident[:])
                    last.then_inc(et_pe, 1)

            def edge_qk(i, m):
                if m == 0:
                    pe.wait_ge(hTe_s, 4 * i + 4)
                if m >= 2:
                    pe.wait_ge(kq_s, 4 * i - 1 + m)
                for side, w in ((0, wk_sb), (1, wq_sb)):
                    for k in range(KC):
                        last = T.matmul(EB[m % 2][:, side * ROWS:(side + 1) * ROWS], w[:, k, m * P:(m + 1) * P],
                                        hT[:, side, k, :], start=(k == 0), stop=(k == KC - 1))
                last.then_inc(qk_pe, 1)

            def edge_scores(i, q, par):
                pe.wait_ge(prod_s, 4 * i + 4)
                pe.wait_ge(hT_s, num(q, par) + 1)
                for m in range(KC):
                    last = T.matmul(SMZ[0:H, 0:ROWS], headsel[:, m, :], prod[:, m, :], start=(m == 0), stop=(m == KC - 1))
                last.then_inc(e_pe, 1)

            def edge_v(i, r):
                pe.wait_ge(kq_s, 4 * i + 3 + r)
                for mm in range(2):
                    m = 2 * r + mm
                    for k in range(KC):
                        last = T.matmul(EB[r][:, mm * ROWS:(mm + 1) * ROWS], wv_sb[:, k, m * P:(m + 1) * P],
                                        hT[:, 0, k, :], start=(k == 0), stop=(k == KC - 1))
                last.then_inc(v_pe, 1)

            def edge_broadcast(i, m):
                if m == 0:
                    pe.wait_ge(sm_c, 5 * i + 5)
                if m < 2:
                    pe.wait_ge(vS_s, 2 * i + 1 + m)
                else:
                    pe.wait_ge(sc_s, 4 * i - 1 + m)
                T.matmul(EB[m % 2][:], headexp[:, m, :], ab[:].rearrange("h s r -> h (s r)"), start=True,
                         stop=True).then_inc(bc_pe, 1)

            def edge_output(k):
                pe.wait_ge(aC_s, k + 1)
                at_least(pe, y_s, 2 * k)
                for j in range(2):
                    for c in range(KC):
                        last = T.matmul(EB[j][:], aC[:, c, j * P:(j + 1) * P], wo_sb[:, c, :], start=(c == 0),
                                        stop=(c == KC - 1))
                last.then_inc(o_pe, 1)

            for t in range(MSTEP0):
                step(*divmod(t, 2), live_at(t))

            def m_body(i):
                q = MSTEP0 // 2 + i
                step(q, 0, e_done=5 * i, gaps={
                    "up": lambda: edge_transpose(i), "xT": lambda: edge_qk(i, 0), "q2T": lambda: edge_qk(i, 1),
                    "z": lambda: edge_qk(i, 2), "down": lambda: edge_qk(i, 3), "f": lambda: edge_scores(i, q, 0)})
                step(q, 1, e_done=5 * i + 2, gaps={
                    "up": lambda: edge_v(i, 0), "xT": lambda: edge_v(i, 1),
                    "f": lambda: [edge_broadcast(i, m) for m in range(KC)]})

            m_body(0)
            with pe.Fori(1, M_ITERS) as i:
                m_body(i)
            with pe.Fori(NSTEP0 // 2, NODE_UNITS // 2) as i:
                for par in range(2):
                    step(i, par)
            pe.wait_ge(wo_in, 16)
            edge_output(0)
            NH = NODE_UNITS // 2
            with pe.Fori(0, F_ITERS) as i:
                for par in range(2):
                    step(NH + i, par, gaps={"f": lambda: edge_output(2 * i + par + 1)})
            step(NH + F_ITERS, 0, gaps={"f": lambda: edge_output(2 * F_ITERS + 1)})
            for t in range(UNITS - 1, UNITS + 3):
                step(*divmod(t, 2), live_at(t))


_INS = ['x', 'src', 'dst', 'L0_gnn_Wq', 'L0_gnn_Wk', 'L0_gnn_Wv', 'L0_gnn_Wo', 'L0_gnn_ln1_g', 'L0_gnn_ln1_b',
        'L0_gnn_ln2_g', 'L0_gnn_ln2_b', 'L0_gnn_W1', 'L0_gnn_b1', 'L0_gnn_W2', 'L0_gnn_b2', 'L0_ffn_w_up',
        'L0_ffn_w_down']


def kernel(**inputs):
    import numpy as _np
    import concourse.bacc as _bacc
    from concourse import mybir as _mybir
    from concourse.bass_utils import run_bass_kernel_spmd as _run

    nc = _bacc.Bacc("TRN2", target_bir_lowering=False, num_devices=1)
    arrays, args = {}, []
    for name in _INS:
        a = _np.ascontiguousarray(inputs[name])
        arrays[f"in_{name}_dram"] = a
        args.append(nc.dram_tensor(f"in_{name}_dram", a.shape, _mybir.dt.from_np(a.dtype), kind="ExternalInput").ap())
    args.append(nc.dram_tensor("out_dram", inputs['x'].shape, _mybir.dt.from_np(_np.dtype('float32')),
                               kind="ExternalOutput").ap())
    gnn_ffn_kernel(nc, *args)
    r = _run(nc, [arrays], core_ids=[0])
    return r.results[0]["out_dram"]
```

```python
import concourse.bass as bass
from concourse import mybir
from contextlib import ExitStack



def gnn_ffn_kernel(nc, x, src, dst, Wq, Wk, Wv, Wo, ln1_g, ln1_b, ln2_g, ln2_b, W1, b1, W2, b2, w_up, w_down, out):
    F32, F32R, BF16, I32 = mybir.dt.float32, mybir.dt.float32r, mybir.dt.bfloat16, mybir.dt.int32
    ALU, ACT, AX = mybir.AluOpType, mybir.ActivationFunctionType, mybir.AxisListType
    P = 128
    N, D = x.shape
    E = src.shape[0]
    H, FF = 8, W1.shape[1]
    KC = D // P
    ROWS = 2 * P
    NODE_UNITS = -(-N // ROWS)
    LAST_BASE = N - ROWS
    EDGE_UNITS = -(-E // ROWS)
    ETILES = 2 * EDGE_UNITS
    EPAD = EDGE_UNITS * ROWS
    UNITS = NODE_UNITS + EDGE_UNITS
    EPS = 1e-5
    MAGIC = 1.5 * 2.0 ** 23
    NEG = -3.0e38
    SKIP = 1 << 20
    MSTEP0 = 4
    MLEN = 3
    M_ITERS = EDGE_UNITS
    NSTEP0 = MSTEP0 + MLEN * (M_ITERS + 1)
    SET_G = 11
    LO = 32
    HP = LO + H
    F_ITERS = (EDGE_UNITS - 2) // 2
    assert NODE_UNITS % 2 == 0 and EDGE_UNITS % 2 == 0 and NSTEP0 < NODE_UNITS and F_ITERS > 2

    es = ExitStack()
    serial = iter(range(1000))
    sb = lambda shape, dt=F32: es.enter_context(nc.sbuf_tensor(f"sb{next(serial)}", shape, dt))
    ps = lambda: es.enter_context(nc.psum_tensor(f"bank{next(serial)}", [P, 512], F32))
    sem = lambda name: es.enter_context(nc.semaphore(name))
    two = lambda shape, dt=F32: [sb(shape, dt), sb(shape, dt)]

    with es:
        ident, ident_bf, ones = sb([P, P]), sb([P, P], BF16), sb([P, P])
        wq_sb, wk_sb, wv_sb = (sb([P, KC, D]) for _ in range(3))
        wo_sb = wk_sb
        w1_sb, w1g, wd_raw = sb([P, KC, FF]), sb([P, KC, 3, FF]), sb([P, KC, FF])
        g1_bc, g2_bc, bln2_bc = sb([P, D]), sb([P, D]), sb([P, D])
        g1_col, bln1_col, b1_col, c1_col = sb([P, KC]), sb([P, KC]), sb([3 * FF, 1]), sb([3 * FF, 1])
        w2e = sb([3 * FF + 2, D], F32R)
        wu_q, wd_q = sb([FF, D], BF16), sb([P, KC, 2, FF], BF16)
        wupT, wdT = sb([P, KC, FF], BF16), sb([2 * FF, D], BF16)
        wsum, ws, wsr, wsu127, wsd127 = sb([P, 2]), sb([P, 2]), sb([P, 2]), sb([P, 1]), sb([P, 1])
        neghalf, negmagic, posmagic = sb([P, 4]), sb([P, 1]), sb([P, 1])
        dst_i, nxt_i, src_i, gdst_i, sct_i = (sb([P, ETILES], I32) for _ in range(5))
        notlast = sb([P, ETILES])
        sbias = sb([HP, EPAD], BF16)
        headsel, headexp = sb([P, KC, HP]), sb([HP, KC, P], F32R)
        xin, xb, x1, res = (two([P, 2, D]) for _ in range(4))
        xn, xg1, s, sg, um, qm = (sb([P, 2, D]) for _ in range(6))
        junk = sb([P, 4, D], BF16)
        w2f, wu_raw, wu_t, w2lo = qm[0:3 * FF + 1, 0, :], qm[0:FF, 1, :], sg[0:FF, 0, :], sg[:, 1, :]
        brow = um[3 * FF:3 * FF + 1, 0, :]
        hexp = [x1[j][0:HP, 0, :].rearrange("h (k c) -> h k c", k=KC) for j in range(2)]
        xT, xqT = sb([P, KC, ROWS]), sb([P, KC, ROWS], BF16)
        hTe = two([3 * FF + 2, ROWS], F32R)
        hfull = sb([2 * FF, ROWS])
        q2, q2T = sb([P, 2, FF], BF16), sb([2 * FF, P], BF16)
        st, mv, tR, R, Rm = two([P, 2, 6]), two([P, 2, 2]), sb([P, 2]), two([P, 2]), two([P, 2])
        mvn = sb([P, 2])
        ssum, mneg, ss2, t2, r2 = two([P, 2]), two([P, 2]), two([P, 2]), sb([P, 2]), two([P, 2])
        xsum, m3neg, ss3, t3, r3 = two([P, 2]), two([P, 2]), two([P, 2]), sb([P, 2]), two([P, 2])
        am, amr, ainv, K, rs1 = sb([P, 2]), sb([P, 2]), sb([P, 2]), two([P, 2]), two([P, 2])
        h1, h2, h3 = (sb([P, 2, FF]) for _ in range(3))
        hmx, hmc, hinv, rs2 = sb([P, 2]), sb([P, 2]), sb([P, 2]), two([P, 2])
        eg = sb([P, 4, D])
        est, emv, etr, er, erm = sb([P, 4, 6]), sb([P, 4, 2]), sb([P, 4]), sb([P, 4]), sb([P, 4])
        emn = sb([P, 4])
        fr = sb([P, ETILES])
        hT = sb([P, 2, KC, ROWS])
        kq, prod, vS, wv = two([P, 2, ROWS]), sb([P, KC, ROWS]), sb([P, KC, ROWS]), two([P, ROWS])
        aT = sb([P, KC, EPAD + 1])
        dstrow_i = aT[0:HP, 0, :].bitcast(I32)
        mx, zz, dd, wc, rz = (sb([HP, ROWS + 1]), sb([HP, ROWS + 1]), sb([HP, 2, ROWS]), sb([HP, 2, ROWS]),
                              sb([HP, ROWS]))
        abf = dd
        ab = sb([HP, 2, ROWS], F32R)
        xg = [eg[:, 0:2, :], eg[:, 2:4, :]]
        y = hT[:, 0].rearrange("p k r -> p (k r)").rearrange("p (j d) -> p j d", j=2)
        aC = [hT[:, 1], wq_sb[:, :, 0:ROWS]]
        res_e = [t[:].rearrange("p k r -> p (k r)").rearrange("p (j d) -> p j d", j=2) for t in (prod, vS)]
        eidx, gidx, sidx = sb([P, 4], I32), two([P, 2], I32), two([P, 2], I32)
        TP, FB, SMQ, SMZ, EB = [ps(), ps()], [ps(), ps()], ps(), ps(), [ps(), ps()]

        wo_in, w_in, l_in, qkv_in, blo_in, set_v, set_g, set_pe, set_a = (sem(n) for n in ("wo_in", "w_in", "l_in", "qkv_in", "blo_in", "set_v", "set_g", "set_pe", "set_a"))
        xload = [sem("xload0"), sem("xload1")]
        odone = [sem("odone0"), sem("odone1")]
        sdone = [sem("sdone0"), sem("sdone1")]
        A_bn, A_mv, R_t, R_s = sem("A_bn"), sem("A_mv"), sem("R_t"), sem("R_s")
        xn_s, xg1_s, xb_s, hlo_s, lists_s = (sem(n) for n in ("xn_s", "xg1_s", "xb_s", "hlo_s", "lists_s"))
        xt_pe, xT_s, z_s, hT_s, f_s = (sem(n) for n in ("xt_pe", "xT_s", "z_s", "hT_s", "f_s"))
        s_s, mneg_s, sq2_s, t2_s, r2_s, sg_s = (sem(n) for n in (
            "s_s", "mneg_s", "sq2_s", "t2_s", "r2_s", "sg_s"))
        x1_s, m3neg_s, um_s, sq3_s, t3_s, r3_s = (sem(n) for n in (
            "x1_s", "m3neg_s", "um_s", "sq3_s", "t3_s", "r3_s"))
        F_c, K_s = sem("F_c"), sem("K_s")
        qm_s, xq_pe, xqT_s, up_s = sem("qm_s"), sem("xq_pe"), sem("xqT_s"), sem("up_s")
        G_c, G_d, q2_s, q2_pe, q2T_s, dn_s, res_s = (sem(n) for n in (
            "G_c", "G_d", "q2_s", "q2_pe", "q2T_s", "dn_s", "res_s"))
        egl, eb_s, emv_s, etr_s, er_s, eh_s = (sem(n) for n in ("egl", "eb_s", "emv_s", "etr_s", "er_s", "eh_s"))
        et_pe, hTe_s, qk_pe, kq_s, prod_s, e_pe = (sem(n) for n in ("et_pe", "eT_s", "qk_pe", "kq_s", "prod_s", "e_pe"))
        sm_c, dd_s, wc_s, abh_s, ab_s, v_pe, vS_s, bc_pe, wv_s, sc_s = (sem(n) for n in (
            "sm_c", "dd_s", "wc_s", "abh_s", "ab_s", "v_pe", "vS_s", "bc_pe", "wv_s", "sc_s"))
        xgl = [sem("xgl0"), sem("xgl1")]
        y_s, aC_s, o_pe = sem("y_s"), [sem("aC0_s"), sem("aC1_s")], sem("o_pe")
        eidx_s, gidx_s, sidx_s = sem("eidx_s"), sem("gidx_s"), sem("sidx_s")
        block = es.enter_context(nc.Block())

        def bc_rows(t, n):
            return t[:].unsqueeze(1).broadcast_to([P, n, D])

        def bc_last(t, n):
            return t[:].unsqueeze(2).broadcast_to([P, 2, n])

        def back(q, par, k):
            n = par - k
            return q + n // 2, n % 2

        def num(q, par):
            return 2 * q + par

        def at_least(eng, sm, value):
            if not (isinstance(value, int) and value <= 0):
                eng.wait_ge(sm, value)

        def m_step(h, r, t):
            c = MLEN * r + t
            return MSTEP0 // 2 + MLEN * h + c // 2, c % 2

        def live_at(step):
            return lambda k: 0 <= step - k < UNITS

        always = lambda k: True
        nothing = lambda: None

        @block.sync
        def _(sp):
            col = lambda v: v.rearrange("(k p) -> p k", p=P)
            mat = lambda m: m.rearrange("(k p) f -> p k f", p=P)
            row = lambda v: v.unsqueeze(0)

            def load(q, par, base):
                u = num(q, par)
                at_least(sp, xn_s, 2 * (u - 1))
                at_least(sp, xb_s, u - 1)
                sp.dma_start(xin[par][:], x[base, :].rearrange("(j p) d -> p j d", p=P)).then_inc(xload[par], 16)

            def store(q, par, lo):
                sp.wait_ge(res_s, 2 * num(q, par) + 2)
                for j in range(2):
                    sp.dma_start(out[lo(j), :], res[par][:, j, :]).then_inc(odone[par], 16)

            rows = lambda q, par: bass.ds((2 * q + par) * ROWS, ROWS)
            orow = lambda q, par: (lambda j: bass.ds((2 * q + par) * ROWS + j * P, P))
            load(0, 0, rows(0, 0))
            load(0, 1, rows(0, 1))
            for t, v in ((w1_sb, mat(W1)), (g1_bc, ln1_g.partition_broadcast(P)), (g2_bc, ln2_g.partition_broadcast(P)),
                         (bln2_bc, ln2_b.partition_broadcast(P)), (g1_col, col(ln1_g)), (bln1_col, col(ln1_b)),
                         (wd_raw, mat(w_down)), (wu_raw, w_up)):
                sp.dma_start(t[:], v, allow_slow_non_contiguous=True).then_inc(w_in, 16)
            for c in range(3):
                sp.dma_start(b1_col[c * FF:(c + 1) * FF, :], b1.rearrange("(p k) -> p k", k=1)).then_inc(w_in, 16)
                sp.dma_start(w2f[c * FF:(c + 1) * FF, :], W2[:, :]).then_inc(w_in, 16)
            sp.dma_start(w2f[3 * FF:, :], row(b2)).then_inc(w_in, 16)
            sp.dma_start(brow, row(ln1_b)).then_inc(w_in, 16)
            sp.wait_ge(set_v, 3)
            full = E // P
            rest = E - full * P
            for t, v in ((dst_i, dst), (src_i, src)):
                sp.dma_start(t[:, 0:full], v[0:full * P].rearrange("(t p) -> p t", p=P),
                             allow_slow_non_contiguous=True).then_inc(l_in, 16)
                sp.dma_start(t[0:rest, full:full + 1], v[full * P:E].rearrange("(p t) -> p t", t=1)).then_inc(l_in, 16)
            sp.dma_start(nxt_i[:, 0:full], dst[1:full * P + 1].rearrange("(t p) -> p t", p=P),
                             allow_slow_non_contiguous=True).then_inc(l_in, 16)
            sp.dma_start(nxt_i[0:rest - 1, full:full + 1],
                         dst[full * P + 1:E].rearrange("(p t) -> p t", t=1)).then_inc(l_in, 16)
            sp.dma_start(dstrow_i[:, 1:E + 1], dst.partition_broadcast(HP)).then_inc(l_in, 16)
            for t, v in ((wk_sb, Wk), (wq_sb, Wq), (wv_sb, Wv)):
                sp.dma_start(t[:], mat(v)).then_inc(qkv_in, 16)

            sp.wait_ge(set_v, 11)
            sp.dma_start(w2e[3 * FF + 1:, :].bitcast(F32), w2lo[3 * FF:3 * FF + 1, :]).then_inc(blo_in, 16)
            for step in range(MSTEP0):
                q, par = divmod(step + 2, 2)
                load(q, par, rows(q, par))
                if step >= 3:
                    q, par = divmod(step - 3, 2)
                    store(q, par, orow(q, par))
            with sp.Fori(MSTEP0 // 2, NODE_UNITS // 2 - 2) as i:
                for par in range(2):
                    load(i + 1, par, rows(i + 1, par))
                    qs, ps_ = back(i, par, 3)
                    store(qs, ps_, orow(qs, ps_))
            h = NODE_UNITS // 2 - 2
            load(h + 1, 0, rows(h + 1, 0))
            sp.wait_ge(qk_pe, 4 * M_ITERS)
            sp.dma_start(wo_sb[:], mat(Wo)).then_inc(wo_in, 16)
            sp.wait_ge(sc_s, 4 * M_ITERS + 4)

            def load_aT(k):
                if k > 1:
                    sp.wait_ge(o_pe, 2 * (k - 1))
                sp.dma_start(aC[k % 2], aT[:, :, k * ROWS + 1:(k + 1) * ROWS + 1]).then_inc(aC_s[k % 2], 16)

            load_aT(0)
            load_aT(1)
            store(*back(h, 0, 3), orow(*back(h, 0, 3)))
            load(h + 1, 1, bass.ds(LAST_BASE, ROWS))
            for u in range(NODE_UNITS - 6, NODE_UNITS):
                q, par = divmod(u, 2)
                if u > NODE_UNITS - 6:
                    load_aT(u - (NODE_UNITS - 7))
                if u < NODE_UNITS - 1:
                    store(q, par, orow(q, par))
                else:
                    sp.wait_ge(odone[0], 32 * (NODE_UNITS // 2))
                    store(q, par, lambda j: bass.ds(LAST_BASE + j * P, P))
            for k in range(7, EDGE_UNITS):
                load_aT(k)

        @block.vector
        def _(dve):
            V = nc.vector
            def edge_lists():
                dve.wait_ge(l_in, 16 * 7)
                V.tensor_tensor(sbias[:], dstrow_i[:, 1:EPAD + 1], dstrow_i[:, 0:EPAD], ALU.not_equal)
                V.tensor_tensor(notlast[:], nxt_i[:], dst_i[:], ALU.is_equal)
                V.tensor_scalar(gdst_i[:], dst_i[:], 0, None, ALU.max).then_inc(lists_s, 1)
                dve.wait_ge(lists_s, 1)
                V.memset(sbias[:, 0:1], 1.0)
                V.memset(aT[:, :, 0:1], 0.0).then_inc(sc_s, 4)
                V.tensor_scalar(notlast[:], notlast[:], float(SKIP), None, ALU.mult).then_inc(lists_s, 1)
                dve.wait_ge(lists_s, 2)
                V.tensor_scalar(sbias[:], sbias[:], NEG, None, ALU.mult)
                V.tensor_tensor(sct_i[:], notlast[:], gdst_i[:], ALU.add).then_inc(lists_s, 1)

            def stage_A(q, par):
                dve.wait_ge(xload[par], 16 * q + 16)
                for j in range(2):
                    V.bn_stats(st[par][:, j, :], xin[par][:, j, :]).then_inc(A_bn, 1)

            def aggregate(q, par):
                u = num(q, par)
                for j in range(2):
                    dve.wait_ge(A_bn, 2 * u + 1 + j)
                    dve.nop(nofuse=True)
                    V.bn_aggr(mv[par][:, j, :], st[par][:, j, :]).then_inc(A_mv, 1)

            def stage_A_edge(q, par, k):
                u = num(q, par)
                dve.wait_ge(xgl[par], 32 * (q - NODE_UNITS // 2) + 32)
                if not isinstance(k, int) or k > 0:
                    dve.wait_ge(xn_s, 2 * u)
                for j in range(2):
                    dve.wait_ge(o_pe, 2 * k + 1 + j)
                    V.scalar_tensor_tensor(y[:, j, :], xg[par][:, j, :], fr[:, bass.ds(2 * k + j, 1)], EB[j][:],
                                           ALU.mult, ALU.add).then_inc(y_s, 1)
                for j in range(2):
                    dve.wait_ge(y_s, 2 * k + 1 + j)
                    V.bn_stats(st[par][:, j, :], y[:, j, :]).then_inc(A_bn, 1)

            def stage_C(q, par, j):
                u = num(q, par)
                if j == 0:
                    dve.wait_ge(xg1_s, u + 1)
                    at_least(dve, sq2_s, 2 * u)
                dve.wait_ge(f_s, 2 * u + 1 + j)
                V.scalar_tensor_tensor(s[:, j, :], FB[j][:], 1.0, xg1[:, j, :], ALU.mult, ALU.add,
                                       accum_out=ssum[par][:, j:j + 1]).then_inc(s_s, 1)

            def s_mean(q, par):
                u = num(q, par)
                dve.wait_ge(s_s, 2 * u + 2)
                V.tensor_scalar(mneg[par][:], ssum[par][:], -1.0 / D, None, ALU.mult).then_inc(mneg_s, 1)

            def stage_D(q, par, j):
                u = num(q, par)
                if j == 0:
                    dve.wait_ge(mneg_s, u + 1)
                    at_least(dve, x1_s, 2 * u)
                V.scalar_tensor_tensor(sg[:, j, :], s[:, j, :], mneg[par][:, j:j + 1], g2_bc[:], ALU.add,
                                       ALU.mult).then_inc(sg_s, 1)

            def stage_E(q, par):
                u = num(q, par)
                dve.wait_ge(sg_s, 2 * u + 2)
                dve.wait_ge(r2_s, u + 1)
                dve.wait_ge(xb_s, u + 1)
                at_least(dve, res_s, 2 * (u - 1))
                for j in range(2):
                    V.scalar_tensor_tensor(x1[par][:, j, :], sg[:, j, :], r2[par][:, j:j + 1], xb[par][:, j, :],
                                           ALU.mult, ALU.add, accum_out=xsum[par][:, j:j + 1]).then_inc(x1_s, 1)

            def x1_mean(q, par):
                u = num(q, par)
                dve.wait_ge(x1_s, 2 * u + 2)
                V.tensor_scalar(m3neg[par][:], xsum[par][:], -1.0 / D, None, ALU.mult).then_inc(m3neg_s, 1)

            def stage_F1(q, par):
                u = num(q, par)
                dve.wait_ge(um_s, 2 * u + 2)
                V.tensor_reduce(am[:], um[:], AX.X, ALU.max, apply_absolute_value=True).then_inc(F_c, 1)

            def stage_F2(q, par, n):
                u = num(q, par)
                dve.wait_ge(F_c, 4 * u + n)
                if n == 1:
                    dve.wait_ge(r3_s, u + 1)
                    V.tensor_tensor(amr[:], am[:], r3[par][:], ALU.mult).then_inc(F_c, 1)
                elif n == 2:
                    V.tensor_scalar(amr[:], amr[:], EPS, None, ALU.max).then_inc(F_c, 1)
                elif n == 3:
                    V.reciprocal(ainv[:], amr[:])
                    V.tensor_scalar(rs1[par][:], amr[:], wsu127[:], None, ALU.mult).then_inc(F_c, 1)
                else:
                    V.scalar_tensor_tensor(K[par][:], ainv[:], 127.0, r3[par][:], ALU.mult, ALU.mult).then_inc(K_s, 1)

            def stage_G(q, par, n):
                u = num(q, par)
                if n == 1:
                    dve.wait_ge(up_s, u + 1)
                elif n < 8:
                    dve.wait_ge(G_c, 6 * u + n - 1)
                if n == 1:
                    V.scalar_tensor_tensor(h1[:], SMQ[:, 0:2 * FF].rearrange("p (j f) -> p j f", j=2), 0.0,
                                           bc_last(rs1[par], FF), ALU.max, ALU.mult).then_inc(G_c, 1)
                elif n == 2:
                    V.tensor_scalar(h2[:], h1[:], 127.0, MAGIC, ALU.min, ALU.add).then_inc(G_c, 1)
                elif n == 3:
                    V.tensor_scalar(h3[:], h2[:], MAGIC, None, ALU.subtract).then_inc(G_c, 1)
                elif n == 4:
                    V.tensor_reduce(hmx[:], h3[:], AX.X, ALU.max).then_inc(G_c, 1)
                elif n == 5:
                    V.tensor_scalar(hmc[:], hmx[:], EPS, None, ALU.max).then_inc(G_c, 1)
                elif n == 6:
                    V.tensor_scalar(rs2[par][:], hmc[:], wsd127[:], None, ALU.mult)
                    V.reciprocal(hinv[:], hmc[:]).then_inc(G_c, 1)
                elif n == 7:
                    V.scalar_tensor_tensor(h1[:], bc_last(hinv, FF), 127.0, h3[:], ALU.mult, ALU.mult).then_inc(G_d, 1)
                else:
                    dve.wait_ge(G_d, u + 1)
                    at_least(dve, q2_pe, u)
                    V.tensor_scalar(q2[:], h1[:], MAGIC, MAGIC, ALU.add, ALU.subtract).then_inc(q2_s, 1)

            def stage_H(q, par, edge):
                u = num(q, par)
                if edge:
                    at_least(dve, sidx_s, u - NODE_UNITS)
                else:
                    at_least(dve, odone[par], 32 * q)
                dest = (res_e if edge else res)[par]
                for j in range(2):
                    dve.wait_ge(dn_s, 2 * u + 1 + j)
                    V.scalar_tensor_tensor(dest[:, j, :], FB[j][:], rs2[par][:, j:j + 1], x1[par][:, j, :],
                                           ALU.mult, ALU.add).then_inc(res_s, 1)

            def hidden_low(q, par):
                u = num(q, par)
                dve.wait_ge(hT_s, 2 * u + 2)
                V.tensor_tensor(hTe[par][FF:2 * FF, :], hfull[FF:, :], hTe[par][FF:2 * FF, :].bitcast(F32),
                                ALU.subtract).then_inc(hlo_s, 1)

            def step(q, par, live=always, k=None, edge_result=False, gaps={}):
                gap = lambda name: gaps.get(name, nothing)()
                unit = lambda n: back(q, par, n)
                run = lambda n, stage, *a: stage(*unit(n), *a) if live(n) else None
                if k is None:
                    run(0, stage_A)
                    gap("stats")
                    run(4, stage_H, edge_result)
                    run(0, aggregate)
                else:
                    run(0, stage_A_edge, k)
                    run(0, aggregate)
                    run(4, stage_H, edge_result)
                gap("A")
                run(2, stage_E)
                run(1, hidden_low)
                run(2, x1_mean)
                gap("E")
                for n in (1, 2, 3):
                    run(3, stage_G, n)
                run(1, stage_C, 0)
                run(3, stage_G, 4)
                run(1, stage_C, 1)
                run(3, stage_G, 5)
                run(1, s_mean)
                run(3, stage_G, 6)
                gap("G6")
                run(3, stage_G, 7)
                gap("G7")
                run(3, stage_G, 8)
                run(2, stage_F1)
                gap("F1")
                run(1, stage_D, 0)
                run(2, stage_F2, 1)
                run(1, stage_D, 1)
                for n in (2, 3, 4):
                    run(2, stage_F2, n)

            def edge_stats(i):
                dve.wait_ge(egl, 64 * i + 64)
                for j in range(4):
                    V.bn_stats(est[:, j, :], eg[:, j, :]).then_inc(eb_s, 1)
                for j in range(4):
                    dve.wait_ge(eb_s, 4 * i + 1 + j)
                    dve.nop(nofuse=True)
                    V.bn_aggr(emv[:, j, :], est[:, j, :]).then_inc(emv_s, 1)

            def edge_exponents(i):
                c = 5 * i
                sbw = sbias[:, bass.ds(i * ROWS, ROWS)]
                e = SMZ[0:HP, 0:ROWS]
                dve.wait_ge(e_pe, i + 1)
                at_least(dve, ab_s, i)
                V.tensor_tensor_scan(mx[:, 1:], sbw, e, mx[:, 0:1], ALU.add, ALU.max).then_inc(sm_c, 1)
                dve.wait_ge(sm_c, c + 1)
                V.tensor_tensor(dd[:, 0, :], e, mx[:, 1:], ALU.subtract).then_inc(dd_s, 1)
                V.tensor_tensor(dd[:, 1, :], mx[:, 0:ROWS], mx[:, 1:], ALU.subtract).then_inc(sm_c, 1)
                dve.wait_ge(sm_c, c + 2)
                V.tensor_tensor(dd[:, 1, :], dd[:, 1, :], sbw, ALU.min).then_inc(dd_s, 1)
                V.tensor_copy(mx[:, 0:1], mx[:, ROWS:ROWS + 1])

            def edge_weights(i):
                c = 5 * i
                dve.wait_ge(wc_s, i + 1)
                V.tensor_tensor_scan(zz[:, 1:], wc[:, 1, :], wc[:, 0, :], zz[:, 0:1], ALU.mult,
                                     ALU.add).then_inc(sm_c, 1)
                dve.wait_ge(sm_c, c + 3)
                V.reciprocal(rz[:], zz[:, 1:])
                V.tensor_tensor(wc[:, 1, :], wc[:, 1, :], zz[:, 0:ROWS], ALU.mult).then_inc(sm_c, 1)
                dve.wait_ge(sm_c, c + 4)
                V.tensor_copy(zz[:, 0:1], zz[:, ROWS:ROWS + 1])
                V.tensor_tensor(abf[:], wc[:], rz[:].unsqueeze(1).broadcast_to([HP, 2, ROWS]),
                                ALU.mult).then_inc(sm_c, 1)

            def edge_low(i):
                dve.wait_ge(abh_s, i + 1)
                V.tensor_tensor(ab[LO:, :, :], abf[LO:, :, :], ab[LO:, :, :].bitcast(F32),
                                ALU.subtract).then_inc(ab_s, 1)

            def edge_weigh(i, m):
                dve.wait_ge(vS_s, 2 * i + 1 + m // 2)
                dve.wait_ge(bc_pe, 4 * i + 1 + m)
                V.tensor_tensor(wv[m % 2][:], EB[m % 2][:, 0:ROWS], vS[:, m, :], ALU.mult).then_inc(wv_s, 1)

            def edge_scan(i, m):
                dve.wait_ge(wv_s, 4 * i + 1 + m)
                V.tensor_tensor_scan(aT[:, m, bass.ds(i * ROWS + 1, ROWS)], EB[m % 2][:, ROWS:2 * ROWS], wv[m % 2][:],
                                     aT[:, m, bass.ds(i * ROWS, 1)], ALU.mult, ALU.add).then_inc(sc_s, 1)

            V.memset(dst_i[:], -1)
            V.memset(nxt_i[:], -1).then_inc(set_v, 1)
            V.memset(src_i[:], 0).then_inc(set_v, 1)
            V.memset(dstrow_i, -1).then_inc(set_v, 1)
            V.memset(ones[:], 1.0)
            V.memset(neghalf[:], -0.5)
            V.memset(negmagic[:], -MAGIC)
            V.memset(mx[:, 0:1], 0.0)
            V.memset(zz[:, 0:1], 0.0)
            for t in hTe:
                V.memset(t[3 * FF:, :].bitcast(F32), 1.0)
            V.memset(wsum[:], 0.0).then_inc(set_v, 1)
            stage_A(0, 0)
            aggregate(0, 0)
            dve.wait_ge(w_in, 16 * 16)
            dve.wait_ge(set_v, 4)
            V.tensor_reduce(wsum[0:FF, 0:1], wu_raw, AX.X, ALU.add, apply_absolute_value=True)
            V.tensor_reduce(wsum[:, 1:2], wd_raw[:].rearrange("p k f -> p (k f)"), AX.X, ALU.add,
                            apply_absolute_value=True).then_inc(set_v, 1)
            brow96 = w2f[3 * FF:, :]
            V.tensor_tensor(brow96, brow96, brow, ALU.add)
            for k in range(KC):
                V.tensor_scalar(w1g[:, k, :, :], w1_sb[:, k, :].unsqueeze(1).broadcast_to([P, 3, FF]),
                                g1_col[:, k:k + 1], None, ALU.mult).then_inc(set_v, 1)
            dve.wait_ge(set_v, 6)
            V.tensor_copy(w2e[0:3 * FF + 1, :], w2f).then_inc(set_v, 1)
            dve.wait_ge(set_v, 10)
            V.tensor_tensor(w2lo[0:3 * FF + 1, :], w2f, w2e[0:3 * FF + 1, :].bitcast(F32),
                            ALU.subtract).then_inc(set_v, 1)
            dve.wait_ge(set_v, 11)
            V.tensor_copy(w2e[2 * FF:3 * FF, :], w2lo[2 * FF:3 * FF, :])
            dve.wait_ge(set_g, SET_G)
            V.tensor_tensor(headexp[:], hexp[0], hexp[1], ALU.add)
            dve.wait_ge(set_pe, 1)
            V.tensor_scalar(ws[:, 0:1], SMQ[:, 0:1], 1.0 / (FF * D), EPS, ALU.mult, ALU.max)
            V.tensor_scalar(ws[:, 1:2], SMQ[:, 1:2], 1.0 / (FF * D), EPS, ALU.mult, ALU.max)
            V.tensor_tensor(c1_col[:], SMZ[0:3 * FF, 0:1], b1_col[:], ALU.add).then_inc(set_v, 1)
            dve.wait_ge(set_v, 12)
            V.reciprocal(wsr[:], ws[:])
            V.tensor_scalar(wsu127[:], ws[:, 0:1], 1.0 / 127.0, None, ALU.mult)
            V.tensor_scalar(wsd127[:], ws[:, 1:2], 1.0 / 127.0, None, ALU.mult).then_inc(set_v, 1)
            dve.wait_ge(set_v, 13)
            wdf = wd_raw[:].rearrange("p k f -> p (k f)")
            V.tensor_scalar(wu_t, wu_raw, wsr[0:FF, 0:1], MAGIC, ALU.mult, ALU.add)
            V.tensor_scalar(wdf, wdf, wsr[:, 1:2], MAGIC, ALU.mult, ALU.add).then_inc(set_v, 1)
            dve.wait_ge(set_v, 14)
            V.tensor_scalar(wu_t, wu_t, MAGIC, 1.0, ALU.subtract, ALU.min)
            V.tensor_scalar(wdf, wdf, MAGIC, 1.0, ALU.subtract, ALU.min).then_inc(set_v, 1)
            dve.wait_ge(set_v, 15)
            V.tensor_scalar(wu_q[:], wu_t, -1.0, None, ALU.max)
            V.tensor_scalar(wd_q[:, :, 0, :], wd_raw[:], -1.0, None, ALU.max)
            V.tensor_scalar(wd_q[:, :, 1, :], wd_raw[:], -1.0, None, ALU.max).then_inc(set_v, 1)

            for t in range(1, MSTEP0):
                step(*divmod(t, 2), live_at(t), gaps={"A": edge_lists if t == 1 else nothing})

            def m_body(h, r, first=False, last=False):
                i = 2 * h + r
                now = lambda f, *a: nothing if last else lambda: f(i, *a)
                before = lambda f, *a: nothing if first else lambda: f(i - 1, *a)
                seq = lambda *fs: lambda: [f() for f in fs]
                step(*m_step(h, r, 0), gaps={"E": now(edge_stats), "F1": before(edge_exponents)})
                step(*m_step(h, r, 1), gaps={"E": before(edge_weights), "F1": before(edge_low)})
                step(*m_step(h, r, 2), gaps={"stats": before(edge_weigh, 0), "A": before(edge_scan, 0),
                                             "E": seq(before(edge_weigh, 1), before(edge_weigh, 2),
                                                      before(edge_scan, 1), before(edge_scan, 2)),
                                             "G6": before(edge_weigh, 3), "G7": before(edge_scan, 3)})

            m_body(0, 0, first=True)
            m_body(0, 1)
            with dve.Fori(1, M_ITERS // 2) as h:
                m_body(h, 0)
                m_body(h, 1)
            m_body(M_ITERS // 2, 0, last=True)
            for t in range(NSTEP0, NODE_UNITS):
                step(*divmod(t, 2))
            for t in range(NODE_UNITS, NODE_UNITS + 4):
                step(*divmod(t, 2), k=t - NODE_UNITS)
            with dve.Fori(2, F_ITERS) as i:
                for par in range(2):
                    step(NODE_UNITS // 2 + i, par, k=2 * i + par, edge_result=True)
            for t in range(UNITS - 2, UNITS + 4):
                step(*divmod(t, 2), live_at(t), k=t - NODE_UNITS, edge_result=True)

        @block.scalar
        def _(act):
            A = nc.scalar
            def normalise(q, par, edge):
                u = num(q, par)
                act.wait_ge(R_s, u + 1)
                at_least(act, xg1_s, u)
                at_least(act, xt_pe, 2 * u)
                rows = y if edge else xin[par]
                for j in range(2):
                    A.activation(xn[:, j, :], rows[:, j, :], ACT.Identity, bias=Rm[par][:, j:j + 1],
                                 scale=R[par][:, j:j + 1]).then_inc(xn_s, 1)

            def quantise(q, par):
                u = num(q, par)
                act.wait_ge(K_s, u + 1)
                at_least(act, xq_pe, 2 * u)
                for j in range(2):
                    A.activation(qm[:, j, :], um[:, j, :], ACT.Identity, bias=posmagic[:],
                                 scale=K[par][:, j:j + 1]).then_inc(qm_s, 1)

            def evict_xqT(q, par):
                u = num(q, par)
                at_least(act, up_s, u)
                for b in range(2):
                    act.wait_ge(xq_pe, 2 * u + 1 + b)
                    A.activation(xqT[:, 2 * b:2 * b + 2, :].rearrange("p k r -> p (k r)"), TP[b][:], ACT.Identity,
                                 bias=negmagic[:]).then_inc(xqT_s, 1)

            def square_s(q, par):
                u = num(q, par)
                act.wait_ge(mneg_s, u + 1)
                for j in range(2):
                    A.activation(junk[:, j, :], s[:, j, :], ACT.Square, bias=mneg[par][:, j:j + 1],
                                 accum_out=ss2[par][:, j:j + 1]).then_inc(sq2_s, 1)

            def centre_x1(q, par):
                u = num(q, par)
                act.wait_ge(m3neg_s, u + 1)
                for j in range(2):
                    A.activation(um[:, j, :], x1[par][:, j, :], ACT.Identity,
                                 bias=m3neg[par][:, j:j + 1]).then_inc(um_s, 1)

            def square_x1(q, par):
                act.wait_ge(m3neg_s, num(q, par) + 1)
                for j in range(2):
                    A.activation(junk[:, 2 + j, :], x1[par][:, j, :], ACT.Square, bias=m3neg[par][:, j:j + 1],
                                 accum_out=ss3[par][:, j:j + 1]).then_inc(sq3_s, 1)

            def evict_xT(q, par):
                u = num(q, par)
                at_least(act, z_s, u)
                for b in range(2):
                    act.wait_ge(xt_pe, 2 * u + 1 + b)
                    A.activation(xT[:, 2 * b:2 * b + 2, :].rearrange("p k r -> p (k r)"), TP[b][:],
                                 ACT.Copy).then_inc(xT_s, 1)

            def evict_q2T(q, par):
                act.wait_ge(q2_pe, num(q, par) + 1)
                at_least(act, dn_s, 2 * num(q, par))
                A.activation(q2T[:], SMQ[0:2 * FF, 64:64 + P // 2].bitcast(BF16), ACT.Copy).then_inc(q2T_s, 1)

            def relu(q, par):
                u = num(q, par)
                act.wait_ge(z_s, u + 1)
                at_least(act, f_s, 2 * (u - 1))
                at_least(act, hlo_s, u)
                A.activation(hTe[par][0:3 * FF, :], SMZ[0:3 * FF, 0:ROWS], ACT.Relu, bias=c1_col[:]).then_inc(hT_s, 1)
                A.activation(hfull[FF:, :], SMZ[FF:2 * FF, 0:ROWS], ACT.Relu, bias=c1_col[FF:2 * FF]).then_inc(hT_s, 1)

            def step(q, par, live=always, edge=False, gaps={}):
                gap = lambda name: gaps.get(name, nothing)()
                run = lambda n, stage, *a: stage(*back(q, par, n), *a) if live(n) else None
                gap("start")
                run(1, relu)
                gap("relu")
                run(3, evict_xqT)
                run(0, normalise, edge)
                gap("xn")
                run(2, square_x1)
                gap("sq3")
                run(2, centre_x1)
                gap("um")
                run(0, evict_xT)
                gap("xT")
                run(3, evict_q2T)
                gap("q2T")
                run(1, square_s)
                gap("sq2")
                run(2, quantise)
                gap("qm")

            def edge_norm(i):
                act.wait_ge(er_s, i + 1)
                for j in range(4):
                    A.activation(eg[:, j, :], eg[:, j, :], ACT.Identity, bias=erm[:, j:j + 1],
                                 scale=er[:, j:j + 1]).then_inc(eh_s, 1)

            def edge_hT(i, r):
                act.wait_ge(et_pe, 4 * i + 1 + r)
                A.activation(hT[:, r // 2, 2 * (r % 2):2 * (r % 2) + 2, :].rearrange("p k r -> p (k r)"),
                             EB[r % 2][:], ACT.Copy).then_inc(hTe_s, 1)

            def edge_kq(i, m):
                act.wait_ge(qk_pe, 4 * i + 1 + m)
                at_least(act, prod_s, 4 * i - 1 + m)
                A.activation(kq[m % 2][:].rearrange("p s r -> p (s r)"), EB[m % 2][:], ACT.Copy).then_inc(kq_s, 1)

            def edge_v(i, r):
                act.wait_ge(v_pe, 2 * i + 1 + r)
                A.activation(vS[:, 2 * r:2 * r + 2, :].rearrange("p k r -> p (k r)"), EB[r][:],
                             ACT.Copy).then_inc(vS_s, 1)

            def edge_exp(i):
                act.wait_ge(dd_s, 2 * i + 2)
                A.activation(wc[:].rearrange("p s r -> p (s r)"), dd[:].rearrange("p s r -> p (s r)"), ACT.Exp,
                             scale=float(D // H) ** -0.5).then_inc(wc_s, 1)

            def edge_high(i):
                act.wait_ge(sm_c, 5 * i + 5)
                at_least(act, bc_pe, 4 * i)
                A.activation(ab[:].rearrange("p s r -> p (s r)"), abf[:].rearrange("p s r -> p (s r)"),
                             ACT.Copy).then_inc(abh_s, 1)

            def weights():
                act.wait_ge(set_pe, 2)
                A.activation(wupT[:].rearrange("p k f -> p (k f)"), TP[0][:, 0:KC * FF // 2].bitcast(BF16), ACT.Copy)
                A.activation(wdT[:], TP[1][0:2 * FF, 0:D // 2].bitcast(BF16), ACT.Copy).then_inc(set_a, 1)

            for t in range(MSTEP0):
                step(*divmod(t, 2), live_at(t), gaps={"xn": weights if t == 0 else nothing})

            def m_body(h, r, first=False, last=False):
                i = 2 * h + r
                now = lambda f, *a: nothing if last else lambda: f(i, *a)
                before = lambda f, *a: nothing if first else lambda: f(i - 1, *a)
                seq = lambda *fs: lambda: [f() for f in fs]
                step(*m_step(h, r, 0), gaps={"start": before(edge_kq, 3), "um": before(edge_v, 0), "xT": now(edge_norm),
                                             "sq2": before(edge_v, 1), "qm": before(edge_exp)})
                step(*m_step(h, r, 1), gaps={"relu": seq(now(edge_hT, 0), now(edge_hT, 1)),
                                             "xn": seq(now(edge_hT, 2), now(edge_hT, 3)), "sq3": before(edge_high),
                                             "q2T": now(edge_kq, 0), "qm": now(edge_kq, 1)})
                step(*m_step(h, r, 2), gaps={"xT": now(edge_kq, 2)})

            m_body(0, 0, first=True)
            m_body(0, 1)
            with act.Fori(1, M_ITERS // 2) as h:
                m_body(h, 0)
                m_body(h, 1)
            m_body(M_ITERS // 2, 0, last=True)
            for t in range(NSTEP0, NODE_UNITS):
                step(*divmod(t, 2))
            with act.Fori(NODE_UNITS // 2, UNITS // 2) as i:
                for par in range(2):
                    step(i, par, edge=True)
            for t in range(UNITS, UNITS + 3):
                step(*divmod(t, 2), live_at(t))

        @block.gpsimd
        def _(pool):
            G = nc.gpsimd
            G.memset(ident[:], 0.0)
            G.memset(headsel[:], 0.0)
            for t in hexp:
                G.memset(t, 1.0)
            G.memset(posmagic[:], MAGIC).then_inc(set_g, 1)
            done = iter(range(1, SET_G))

            def select(t, compare_op, fill, base, pattern, channel_multiplier):
                pool.wait_ge(set_g, next(done))
                G.affine_select(out=t, in_=t, compare_op=compare_op, fill=fill, base=base, pattern=pattern,
                                channel_multiplier=channel_multiplier).then_inc(set_g, 1)

            select(ident[:], ALU.not_equal, 1.0, 0, [[-1, P]], 1)
            half = P // 2
            for r in range(2):
                for c in (0, LO):
                    select(headsel[r * half:(r + 1) * half, :, c:c + H], ALU.not_equal, 1.0, -r, [[-2, KC], [1, H]], 0)
            for c, t in enumerate(hexp):
                select(t, ALU.is_ge, 0.0, half * c * LO, [[P, KC], [1, P]], -half)
                select(t, ALU.is_ge, 0.0, half - 1 - half * c * LO, [[-P, KC], [-1, P]], half)
            pool.wait_ge(set_g, next(done))
            G.tensor_copy(ident_bf[:], ident[:]).then_inc(set_g, 1)

            def rows_scale(q, par, node):
                u = num(q, par)
                pool.wait_ge(A_mv, 2 * u + 2)
                pool.nop(nofuse=True)
                if node:
                    G.tensor_scalar(tR[:], mv[par][:, :, 1], 1.0 + EPS, EPS * EPS, ALU.mult, ALU.add).then_inc(R_t, 1)
                else:
                    G.tensor_scalar(tR[:], mv[par][:, :, 1], 1.0, EPS, ALU.mult, ALU.add).then_inc(R_t, 1)
                G.tensor_scalar(mvn[:], mv[par][:, :, 0], -1.0, 0.0, ALU.mult, ALU.add)
                pool.wait_ge(R_t, 2 * u + 1)
                G.tensor_tensor(R[par][:], tR[:], neghalf[:, 0:2], ALU.pow).then_inc(R_t, 1)
                pool.wait_ge(R_t, 2 * u + 2)
                G.tensor_tensor(Rm[par][:], mvn[:], R[par][:], ALU.mult).then_inc(R_s, 1)

            def add_b(q, par, rows):
                u = num(q, par)
                at_least(pool, x1_s, 2 * (u - 1))
                G.tensor_tensor(xb[par][:], rows[par][:], bc_rows(bln2_bc, 2), ALU.add).then_inc(xb_s, 1)

            def s_scale(q, par):
                u = num(q, par)
                pool.wait_ge(sq2_s, 2 * u + 2)
                pool.nop(nofuse=True)
                G.tensor_scalar(t2[:], ss2[par][:], 1.0 / D, EPS, ALU.mult, ALU.add).then_inc(t2_s, 1)
                pool.wait_ge(t2_s, u + 1)
                G.tensor_tensor(r2[par][:], t2[:], neghalf[:, 0:2], ALU.pow).then_inc(r2_s, 1)

            def gain1(q, par):
                u = num(q, par)
                pool.wait_ge(xn_s, 2 * u + 2)
                at_least(pool, s_s, 2 * u)
                G.tensor_tensor(xg1[:], xn[:], bc_rows(g1_bc, 2), ALU.mult).then_inc(xg1_s, 1)

            def x1_scale(q, par):
                u = num(q, par)
                pool.wait_ge(sq3_s, 2 * u + 2)
                pool.nop(nofuse=True)
                G.tensor_scalar(t3[:], ss3[par][:], 1.0 / D, EPS, ALU.mult, ALU.add).then_inc(t3_s, 1)
                pool.wait_ge(t3_s, u + 1)
                G.tensor_tensor(r3[par][:], t3[:], neghalf[:, 0:2], ALU.pow).then_inc(r3_s, 1)

            def step(q, par, live=always, k=None, gaps={}):
                gap = lambda name: gaps.get(name, nothing)()
                run = lambda n, stage, *a: stage(*back(q, par, n), *a) if live(n) else None
                gap("start")
                run(1, gain1)
                run(2, s_scale)
                run(0, rows_scale, k is None)
                gap("R")
                run(1, add_b, xin if k is None or k == 0 else xg)
                gap("b")
                run(2, x1_scale)
                gap("r3")

            def gather_edges(i):
                at_least(pool, et_pe, 4 * i)
                G.tensor_copy(eidx[:, 0:2], src_i[:, bass.ds(2 * i, 2)])
                G.tensor_copy(eidx[:, 2:4], gdst_i[:, bass.ds(2 * i, 2)]).then_inc(eidx_s, 1)
                pool.wait_ge(eidx_s, i + 1)
                pool.nop(nofuse=True)
                for t in range(4):
                    G.indirect_dma_start(eg[:, t, :], None, x[:, :],
                                         bass.IndirectOffsetOnAxis(ap=eidx[:, t:t + 1], axis=0)).then_inc(egl, 16)

            def edge_scale(i):
                pool.wait_ge(emv_s, 4 * i + 4)
                pool.nop(nofuse=True)
                G.tensor_scalar(emn[:], emv[:, :, 0], -1.0, 0.0, ALU.mult, ALU.add)
                G.tensor_scalar(etr[:], emv[:, :, 1], 1.0, EPS, ALU.mult, ALU.add).then_inc(etr_s, 1)
                pool.wait_ge(etr_s, 2 * i + 1)
                G.tensor_tensor(er[:], etr[:], neghalf[:], ALU.pow).then_inc(etr_s, 1)
                pool.wait_ge(etr_s, 2 * i + 2)
                G.tensor_copy(fr[:, bass.ds(2 * i, 2)], er[:, 2:4])
                G.tensor_tensor(erm[:], emn[:], er[:], ALU.mult).then_inc(er_s, 1)

            def edge_prod(i, m):
                pool.wait_ge(kq_s, 4 * i + 1 + m)
                at_least(pool, e_pe, i)
                G.tensor_tensor(prod[:, m, :], kq[m % 2][:, 0, :], kq[m % 2][:, 1, :], ALU.mult).then_inc(prod_s, 1)

            def gather_dst(par, k):
                G.tensor_copy(gidx[par][:], gdst_i[:, bass.ds(2 * k, 2)]).then_inc(gidx_s, 1)
                pool.wait_ge(gidx_s, k + 1)
                pool.nop(nofuse=True)
                for j in range(2):
                    G.indirect_dma_start(xg[par][:, j, :], None, x[:, :],
                                         bass.IndirectOffsetOnAxis(ap=gidx[par][:, j:j + 1], axis=0)
                                         ).then_inc(xgl[par], 16)

            def scatter(h, par):
                k = 2 * h + par
                pool.wait_ge(res_s, 2 * (NODE_UNITS + k) + 2)
                at_least(pool, sdone[1 - par], 32 * (h + par))
                G.tensor_copy(sidx[par][:], sct_i[:, bass.ds(2 * k, 2)]).then_inc(sidx_s, 1)
                pool.wait_ge(sidx_s, k + 1)
                pool.nop(nofuse=True)
                for j in range(2):
                    G.indirect_dma_start(out[:, :], bass.IndirectOffsetOnAxis(ap=sidx[par][:, j:j + 1], axis=0),
                                         res_e[par][:, j, :], None, bounds_check=N - 1,
                                         oob_is_err=False).then_inc(sdone[par], 16)

            pool.wait_ge(set_v, 4)
            step(0, 0, live_at(0))
            pool.wait_ge(set_v, 16)
            for t in range(1, MSTEP0):
                step(*divmod(t, 2), live_at(t))
            pool.wait_ge(lists_s, 3)
            gather_edges(0)

            def m_body(h, r, first=False, last=False, more=True):
                i = 2 * h + r
                now = lambda f, *a: nothing if last else lambda: f(i, *a)
                before = lambda f, *a: nothing if first else lambda: f(i - 1, *a)
                seq = lambda *fs: lambda: [f() for f in fs]
                step(*m_step(h, r, 0), gaps={"R": before(edge_prod, 2), "b": before(edge_prod, 3)})
                step(*m_step(h, r, 1), gaps={"start": now(edge_scale), "r3": now(edge_prod, 0)})
                step(*m_step(h, r, 2), gaps={"r3": seq((lambda: gather_edges(i + 1)) if more else nothing,
                                                       now(edge_prod, 1))})

            m_body(0, 0, first=True)
            m_body(0, 1)
            with pool.Fori(1, M_ITERS // 2 - 1) as h:
                m_body(h, 0)
                m_body(h, 1)
            m_body(M_ITERS // 2 - 1, 0)
            m_body(M_ITERS // 2 - 1, 1, more=False)
            m_body(M_ITERS // 2, 0, last=True, more=False)
            pool.wait_ge(et_pe, 4 * M_ITERS)
            gather_dst(0, 0)
            gather_dst(1, 1)
            for t in range(NSTEP0, NODE_UNITS):
                step(*divmod(t, 2))
            NH = NODE_UNITS // 2

            for k in range(EDGE_UNITS + 4):
                h, par = divmod(k, 2)

                def write():
                    if k == 4:
                        pool.wait_ge(odone[0], 32 * (NODE_UNITS // 2))
                        pool.wait_ge(odone[1], 32 * (NODE_UNITS // 2))
                    if k >= 4:
                        scatter(h - 2, par)

                def gather():
                    if 1 <= k < EDGE_UNITS - 1:
                        pool.wait_ge(xb_s, NODE_UNITS + k)
                        gather_dst(1 - par, k + 1)

                step(NH + h, par, live_at(NODE_UNITS + k), k=k, gaps={"b": gather, "r3": write})
            for par in range(2):
                pool.wait_ge(sdone[par], 32 * (EDGE_UNITS // 2))

        @block.tensor
        def _(pe):
            T = nc.tensor
            pe.wait_ge(set_g, SET_G)
            pe.wait_ge(set_v, 9)
            T.matmul(SMQ[:, 0:2], ones[:], wsum[:], start=True, stop=True)
            for c in range(3):
                for k in range(KC):
                    last = T.matmul(SMZ[c * FF:(c + 1) * FF, 0:1], w1_sb[:, k, :], bln1_col[:, k:k + 1], start=(k == 0),
                                    stop=(k == KC - 1))
            last.then_inc(set_pe, 1)
            pe.wait_ge(set_v, 16)
            for k in range(KC):
                T.transpose(TP[0][:, k * FF // 2:(k + 1) * FF // 2].bitcast(BF16), wu_q[:, k * P:(k + 1) * P],
                            ident_bf[0:FF, 0:FF])
            for k in range(KC):
                last = T.transpose(TP[1][0:2 * FF, k * P // 2:(k + 1) * P // 2].bitcast(BF16),
                                   wd_q[:, k, :, :].rearrange("p a f -> p (a f)"), ident_bf[:])
            last.then_inc(set_pe, 1)
            pe.wait_ge(set_a, 1)

            def transpose_rows(rows, count):
                for b in range(2):
                    yield b
                    for kk in range(2):
                        k = 2 * b + kk
                        for j in range(2):
                            last = T.transpose(TP[b][:, kk * ROWS + j * P:kk * ROWS + (j + 1) * P],
                                               rows[:, j, k * P:(k + 1) * P], ident[:])
                    last.then_inc(count, 1)

            def transpose_xq(q, par):
                u = num(q, par)
                pe.wait_ge(qm_s, 2 * u + 2)
                for b in transpose_rows(qm, xq_pe):
                    pe.wait_ge(xT_s, 2 * min_unit(u + 2) + 1 + b)

            def up(q, par):
                u = num(q, par)
                pe.wait_ge(xqT_s, 2 * u + 2)
                at_least(pe, q2T_s, u)
                for j in range(2):
                    for k in range(KC):
                        last = T.matmul(SMQ[:, j * FF:(j + 1) * FF], xqT[:, k, j * P:(j + 1) * P], wupT[:, k, :],
                                        start=(k == 0), stop=(k == KC - 1))
                last.then_inc(up_s, 1)

            def transpose_x(q, par, quant):
                u = num(q, par)
                pe.wait_ge(xn_s, 2 * u + 2)
                for b in transpose_rows(xn, xt_pe):
                    if quant:
                        pe.wait_ge(xqT_s, 2 * (u - 3) + 1 + b)
                    else:
                        at_least(pe, xT_s, 2 * (u - 1) + 1 + b)

            def transpose_q2(q, par):
                u = num(q, par)
                pe.wait_ge(q2_s, u + 1)
                pe.nop(nofuse=True)
                T.transpose(SMQ[0:2 * FF, 64:64 + P // 2].bitcast(BF16), q2[:].rearrange("p j f -> p (j f)"),
                            ident_bf[:]).then_inc(q2_pe, 1)

            def hidden(q, par, scores):
                u = num(q, par)
                pe.wait_ge(xT_s, 2 * u + 2)
                at_least(pe, hT_s, 2 * u)
                if scores is not None:
                    pe.wait_ge(sm_c, 5 * scores + 2)
                for k in range(KC):
                    last = T.matmul(SMZ[0:3 * FF, 0:ROWS], w1g[:, k, :, :].rearrange("p c f -> p (c f)"), xT[:, k, :],
                                    start=(k == 0), stop=(k == KC - 1))
                last.then_inc(z_s, 1)

            def down(q, par):
                u = num(q, par)
                pe.wait_ge(q2T_s, u + 1)
                pe.wait_ge(s_s, 2 * min_unit(u + 2) + 2)
                for j in range(2):
                    T.matmul(FB[j][:], q2T[j * FF:(j + 1) * FF, :], wdT[j * FF:(j + 1) * FF, :], start=True,
                             stop=True).then_inc(dn_s, 1)

            def ffn(q, par, after_down):
                u = num(q, par)
                pe.wait_ge(hlo_s, u + 1)
                for j in range(2):
                    if after_down:
                        pe.wait_ge(res_s, 2 * (u - 3) + 1 + j)
                    else:
                        at_least(pe, s_s, 2 * (u - 1) + 1 + j)
                    T.matmul(FB[j][:], hTe[par][:, j * P:(j + 1) * P], w2e[:], start=True, stop=True).then_inc(f_s, 1)

            def min_unit(u):
                return min(u, UNITS - 1) if isinstance(u, int) else u

            def step(q, par, live=always, scores=None, gaps={}):
                gap = lambda name: gaps.get(name, nothing)()
                run = lambda n, stage, *a: stage(*back(q, par, n), *a) if live(n) else None
                run(1, hidden, scores)
                gap("z")
                run(3, transpose_xq)
                gap("xqT")
                run(3, up)
                gap("up")
                run(1, ffn, live(4))
                gap("f")
                run(0, transpose_x, live(3))
                gap("xT")
                run(3, transpose_q2)
                gap("q2T")
                run(3, down)
                gap("down")

            def edge_transpose(i, r):
                side, b = divmod(r, 2)
                pe.wait_ge(eh_s, 4 * i + (2 if side == 0 else 4))
                if r < 2:
                    at_least(pe, vS_s, 2 * (i - 1) + 1 + r)
                else:
                    pe.wait_ge(hTe_s, 4 * i - 1 + r)
                for kk in range(2):
                    k = 2 * b + kk
                    for j in range(2):
                        last = T.transpose(EB[r % 2][:, kk * ROWS + j * P:kk * ROWS + (j + 1) * P],
                                           eg[:, 2 * side + j, k * P:(k + 1) * P], ident[:])
                last.then_inc(et_pe, 1)

            def edge_qk(i, m, first):
                if m == 0:
                    pe.wait_ge(hTe_s, 4 * i + 4)
                elif m >= 2 and first:
                    pe.wait_ge(kq_s, 4 * i - 1 + m)
                elif m >= 2:
                    pe.wait_ge(sc_s, 4 * i + 1 + m)
                for side, w in ((0, wk_sb), (1, wq_sb)):
                    for k in range(KC):
                        last = T.matmul(EB[m % 2][:, side * ROWS:(side + 1) * ROWS], w[:, k, m * P:(m + 1) * P],
                                        hT[:, side, k, :], start=(k == 0), stop=(k == KC - 1))
                last.then_inc(qk_pe, 1)

            def edge_scores(g, q, par):
                pe.wait_ge(prod_s, 4 * g + 4)
                pe.wait_ge(hT_s, 2 * num(q, par))
                for m in range(KC):
                    last = T.matmul(SMZ[0:HP, 0:ROWS], headsel[:, m, :], prod[:, m, :], start=(m == 0), stop=(m == KC - 1))
                last.then_inc(e_pe, 1)

            def edge_v(g, r):
                pe.wait_ge(kq_s, 4 * g + 3 + r)
                for mm in range(2):
                    m = 2 * r + mm
                    for k in range(KC):
                        last = T.matmul(EB[r][:, mm * ROWS:(mm + 1) * ROWS], wv_sb[:, k, m * P:(m + 1) * P],
                                        hT[:, 0, k, :], start=(k == 0), stop=(k == KC - 1))
                last.then_inc(v_pe, 1)

            def edge_broadcast(g, m, last):
                if m == 0:
                    pe.wait_ge(ab_s, g + 1)
                if m < 2 and last:
                    pe.wait_ge(vS_s, 2 * g + 1 + m)
                elif m < 2:
                    pe.wait_ge(kq_s, 4 * g + 5 + m)
                else:
                    pe.wait_ge(sc_s, 4 * g + 3 + m)
                T.matmul(EB[m % 2][:], headexp[:, m, :], ab[:].rearrange("h s r -> h (s r)"), start=True,
                         stop=True).then_inc(bc_pe, 1)

            def edge_output(h, par, j):
                k = num(h, par)
                if j == 0:
                    pe.wait_ge(aC_s[par], 16 * h + 16)
                at_least(pe, y_s, 2 * (k - 1) + 1 + j)
                for c in range(KC):
                    last = T.matmul(EB[j][:], aC[par][:, c, j * P:(j + 1) * P], wo_sb[:, c, :], start=(c == 0),
                                    stop=(c == KC - 1))
                last.then_inc(o_pe, 1)

            def output_gaps(h, par):
                return {"xqT": lambda: edge_output(h, par, 0), "xT": lambda: edge_output(h, par, 1)}

            for t in range(MSTEP0):
                step(*divmod(t, 2), live_at(t), gaps={"up": (lambda: pe.wait_ge(blo_in, 16)) if t == 1 else nothing})

            def m_body(h, r, first=False, last=False):
                i = 2 * h + r
                now = lambda f, *a: nothing if last else lambda: f(i, *a)
                before = lambda f, *a: nothing if first else lambda: f(i - 1, *a)
                seq = lambda *fs: lambda: [f() for f in fs]
                step(*m_step(h, r, 0), gaps={"xqT": before(edge_v, 0), "xT": before(edge_scores, *m_step(h, r, 0)),
                                             "q2T": before(edge_v, 1)})
                step(*m_step(h, r, 1), scores=None if first else i - 1, gaps={
                    "z": seq(now(edge_transpose, 0), now(edge_transpose, 1)),
                    "xqT": seq(now(edge_transpose, 2), now(edge_transpose, 3)),
                    "xT": now(edge_qk, 0, first), "q2T": now(edge_qk, 1, first),
                    "down": before(edge_broadcast, 0, last)})
                step(*m_step(h, r, 2), gaps={
                    "xqT": before(edge_broadcast, 1, last), "up": before(edge_broadcast, 2, last),
                    "f": before(edge_broadcast, 3, last), "xT": now(edge_qk, 2, first), "q2T": now(edge_qk, 3, first)})

            m_body(0, 0, first=True)
            m_body(0, 1)
            with pe.Fori(1, M_ITERS // 2) as h:
                m_body(h, 0)
                m_body(h, 1)
            m_body(M_ITERS // 2, 0, last=True)
            for t in range(NSTEP0, NODE_UNITS - 1):
                step(*divmod(t, 2))
            NH = NODE_UNITS // 2
            step(NH - 1, 1, gaps=dict(output_gaps(0, 0), z=lambda: pe.wait_ge(wo_in, 16)))
            with pe.Fori(0, F_ITERS) as i:
                for par in range(2):
                    step(NH + i, par, gaps=output_gaps(i + par, 1 - par))
            step(NH + F_ITERS, 0, gaps=output_gaps(F_ITERS, 1))
            for t in range(UNITS - 1, UNITS + 3):
                step(*divmod(t, 2), live_at(t))


_INS = ['x', 'src', 'dst', 'L0_gnn_Wq', 'L0_gnn_Wk', 'L0_gnn_Wv', 'L0_gnn_Wo', 'L0_gnn_ln1_g', 'L0_gnn_ln1_b',
        'L0_gnn_ln2_g', 'L0_gnn_ln2_b', 'L0_gnn_W1', 'L0_gnn_b1', 'L0_gnn_W2', 'L0_gnn_b2', 'L0_ffn_w_up',
        'L0_ffn_w_down']


def kernel(**inputs):
    import numpy as _np
    import concourse.bacc as _bacc
    from concourse import mybir as _mybir
    from concourse.bass_utils import run_bass_kernel_spmd as _run

    nc = _bacc.Bacc("TRN2", target_bir_lowering=False, num_devices=1)
    arrays, args = {}, []
    for name in _INS:
        a = _np.ascontiguousarray(inputs[name])
        arrays[f"in_{name}_dram"] = a
        args.append(nc.dram_tensor(f"in_{name}_dram", a.shape, _mybir.dt.from_np(a.dtype), kind="ExternalInput").ap())
    args.append(nc.dram_tensor("out_dram", inputs['x'].shape, _mybir.dt.from_np(_np.dtype('float32')),
                               kind="ExternalOutput").ap())
    gnn_ffn_kernel(nc, *args)
    r = _run(nc, [arrays], core_ids=[0])
    return r.results[0]["out_dram"]
```
